# Optimizing a Trainium2 kernel written in Bass

```python
import numpy as np
import jax
import jax.numpy as jnp

def _softmax(x, axis=-1):
    return jax.nn.softmax(x, axis=axis)

def _gelu(x):
    return jax.nn.gelu(x, approximate=True)

def _silu(x):
    return jax.nn.silu(x)

def _sigmoid(x):
    return jax.nn.sigmoid(x)

def _layernorm(x, axis=-1, eps=1e-05):
    m = jnp.mean(x, axis=axis, keepdims=True)
    v = jnp.var(x, axis=axis, keepdims=True)
    return (x - m) / jnp.sqrt(v + eps)

def _scatter_add(tgt, idx, src, axis=0):
    return tgt.at[idx].add(src)

def _segment_sum(src, seg, n):
    return jax.ops.segment_sum(src, seg, n)
kernel_name = 'mk_adj_resnorm_d4_adj_r2_ae9533'

def setup_inputs(seed: int=0):
    np.random.seed(seed)
    _w = jnp.asarray

    def _rec_inputs():
        import jax
        import jax.numpy as jnp
        _gk = jax.random.key(seed)
        x = 7.34e-05 + 1 * jax.random.normal(jax.random.fold_in(_gk, 1), (128, 128, 256), jnp.float32)
        _a = jax.random.bernoulli(jax.random.fold_in(_gk, 2), 0.03125, (128, 128))
        _a = jnp.logical_or(_a, jnp.swapaxes(_a, -1, -2))
        _a = jnp.logical_or(_a, jnp.eye(128, dtype=bool))
        _af = _a.astype(jnp.float32)
        adj = _af
        return (x, adj)
    x, adj = _rec_inputs()

    def _L0_gnn_setup():
        import jax, jax.numpy as jnp
        import numpy as np
        B, N, D, H = (16, 1025, 256, 8)
        LN_EPS = 1e-05

        def _make_mask(key, n):
            n_proto = n - 1
            adj = jax.random.bernoulli(key, 0.03, (n_proto, n_proto)).astype(jnp.float32)
            adj = jnp.clip(adj + adj.T + jnp.eye(n_proto, dtype=jnp.float32), 0.0, 1.0)
            mask = jnp.zeros((n, n), dtype=jnp.float32)
            mask = mask.at[0, :].set(1.0).at[:, 0].set(1.0)
            mask = mask.at[1:, 1:].set(adj)
            return mask
        key = jax.random.key(seed)
        ks = jax.random.split(key, 7)
        s = 1.0 / np.sqrt(D)
        return {'x': jax.random.normal(ks[0], (B, N, D), dtype=jnp.float32), 'w_qkv': jax.random.uniform(ks[1], (D, 3 * D), dtype=jnp.float32, minval=-s, maxval=s), 'w_proj': jax.random.uniform(ks[2], (D, D), dtype=jnp.float32, minval=-s, maxval=s), 'b_proj': jnp.zeros((D,), dtype=jnp.float32), 'ln_gamma': jnp.ones((D,), dtype=jnp.float32), 'ln_beta': jnp.zeros((D,), dtype=jnp.float32), 'attn_mask': _make_mask(ks[3], N)}
    _L0_gnn_all = _L0_gnn_setup()
    _L0_gnn_in = {k: v for k, v in _L0_gnn_all.items() if k in ('w_qkv', 'w_proj', 'b_proj', 'ln_gamma', 'ln_beta')}
    del _L0_gnn_all

    def _L1_gnn_setup():
        import jax, jax.numpy as jnp
        import numpy as np
        B, N, D, H = (4, 1024, 256, 8)
        HD = D // H
        key = jax.random.key(seed)
        ks = jax.random.split(key, 10)
        x = jax.random.normal(ks[0], (B, N, D), dtype=jnp.float32)
        adj = (jax.random.uniform(ks[1], (N, N)) < 0.1).astype(jnp.float32)
        s = 1.0 / np.sqrt(D)
        Wq = jax.random.normal(ks[2], (D, D), dtype=jnp.float32) * s
        Wk = jax.random.normal(ks[3], (D, D), dtype=jnp.float32) * s
        Wv = jax.random.normal(ks[4], (D, D), dtype=jnp.float32) * s
        Wo = jax.random.normal(ks[5], (D, D), dtype=jnp.float32) * s
        bq = jnp.zeros((D,), jnp.float32)
        bk = jnp.zeros((D,), jnp.float32)
        bv = jnp.zeros((D,), jnp.float32)
        bo = jnp.zeros((D,), jnp.float32)
        return {'x': x, 'adj': adj, 'Wq': Wq, 'bq': bq, 'Wk': Wk, 'bk': bk, 'Wv': Wv, 'bv': bv, 'Wo': Wo, 'bo': bo}
    _L1_gnn_all = _L1_gnn_setup()
    _L1_gnn_in = {k: v for k, v in _L1_gnn_all.items() if k in ('Wq', 'bq', 'Wk', 'bk', 'Wv', 'bv', 'Wo', 'bo')}
    del _L1_gnn_all

    def _L2_gnn_setup():
        import jax, jax.numpy as jnp
        import numpy as np
        B, N, F_IN, F_OUT = (16, 1024, 256, 256)
        key = jax.random.key(seed)
        k1, k2, k3 = jax.random.split(key, 3)
        x = jax.random.normal(k1, (B, N, F_IN), dtype=jnp.float32)
        adj = jax.random.uniform(k2, (N, N), dtype=jnp.float32)
        bound = np.sqrt(6.0 / F_OUT)
        weight = jax.random.uniform(k3, (F_IN, F_OUT), dtype=jnp.float32, minval=-bound, maxval=bound)
        bias = jnp.zeros((F_OUT,), dtype=jnp.float32)
        return {'x': x, 'adj': adj, 'weight': weight, 'bias': bias}
    _L2_gnn_all = _L2_gnn_setup()
    _L2_gnn_in = {k: v for k, v in _L2_gnn_all.items() if k in ('weight', 'bias')}
    del _L2_gnn_all

    def _L3_gnn_setup():
        import jax, jax.numpy as jnp
        import numpy as np
        key = jax.random.key(seed)
        k1, k2, k3, k4 = jax.random.split(key, 4)
        B, D, N = (4, 128, 256)
        scale = 1.0 / np.sqrt(2 * D)
        x = jax.random.normal(k1, (B, D, N), dtype=jnp.float32)
        W1 = jax.random.normal(k2, (D, D), dtype=jnp.float32) * scale
        W2 = jax.random.normal(k3, (D, D), dtype=jnp.float32) * scale
        b = jax.random.normal(k4, (D,), dtype=jnp.float32) * scale
        return {'x': x, 'W1': W1, 'W2': W2, 'b': b}
    _L3_gnn_all = _L3_gnn_setup()
    _L3_gnn_in = {k: v for k, v in _L3_gnn_all.items() if k in ('b',)}
    del _L3_gnn_all
    return {'x': x, 'adj': adj, 'L0_gnn_w_qkv': _L0_gnn_in['w_qkv'], 'L0_gnn_w_proj': _L0_gnn_in['w_proj'], 'L0_gnn_b_proj': _L0_gnn_in['b_proj'], 'L0_gnn_ln_gamma': _L0_gnn_in['ln_gamma'], 'L0_gnn_ln_beta': _L0_gnn_in['ln_beta'], 'L1_gnn_Wq': _L1_gnn_in['Wq'], 'L1_gnn_bq': _L1_gnn_in['bq'], 'L1_gnn_Wk': _L1_gnn_in['Wk'], 'L1_gnn_bk': _L1_gnn_in['bk'], 'L1_gnn_Wv': _L1_gnn_in['Wv'], 'L1_gnn_bv': _L1_gnn_in['bv'], 'L1_gnn_Wo': _L1_gnn_in['Wo'], 'L1_gnn_bo': _L1_gnn_in['bo'], 'L2_gnn_weight': _L2_gnn_in['weight'], 'L2_gnn_bias': _L2_gnn_in['bias'], 'L3_gnn_b': _L3_gnn_in['b']}

def reference(x, adj, L0_gnn_w_qkv, L0_gnn_w_proj, L0_gnn_b_proj, L0_gnn_ln_gamma, L0_gnn_ln_beta, L1_gnn_Wq, L1_gnn_bq, L1_gnn_Wk, L1_gnn_bk, L1_gnn_Wv, L1_gnn_bv, L1_gnn_Wo, L1_gnn_bo, L2_gnn_weight, L2_gnn_bias, L3_gnn_b):
    import jax
    import jax.numpy as jnp

    def _L0_gnn_ref(x, w_qkv, w_proj, b_proj, ln_gamma, ln_beta, attn_mask):
        import jax, jax.numpy as jnp
        import numpy as np
        B, N, D, H = (16, 1025, 256, 8)
        LN_EPS = 1e-05

        def _make_mask(key, n):
            n_proto = n - 1
            adj = jax.random.bernoulli(key, 0.03, (n_proto, n_proto)).astype(jnp.float32)
            adj = jnp.clip(adj + adj.T + jnp.eye(n_proto, dtype=jnp.float32), 0.0, 1.0)
            mask = jnp.zeros((n, n), dtype=jnp.float32)
            mask = mask.at[0, :].set(1.0).at[:, 0].set(1.0)
            mask = mask.at[1:, 1:].set(adj)
            return mask
        b, n, d = x.shape
        hd = d // H
        scale = hd ** (-0.5)
        qkv = (x @ w_qkv).reshape(b, n, 3, H, hd).transpose(2, 0, 3, 1, 4)
        q, k, v = (qkv[0], qkv[1], qkv[2])
        attn = jnp.einsum('bhnd,bhmd->bhnm', q, k) * scale
        attn = jnp.where(attn_mask[None, None] == 0, -jnp.inf, attn)
        attn = jax.nn.softmax(attn, axis=-1)
        o = jnp.einsum('bhnm,bhmd->bhnd', attn, v).transpose(0, 2, 1, 3).reshape(b, n, d)
        o = o @ w_proj + b_proj
        mu = jnp.mean(o, axis=-1, keepdims=True)
        var = jnp.mean(jnp.square(o - mu), axis=-1, keepdims=True)
        ln = (o - mu) * jax.lax.rsqrt(var + LN_EPS) * ln_gamma + ln_beta
        return o + ln

    def _L1_gnn_ref(x, adj, Wq, bq, Wk, bk, Wv, bv, Wo, bo):
        import jax, jax.numpy as jnp
        import numpy as np
        B, N, D, H = (4, 1024, 256, 8)
        HD = D // H
        b, n, d = x.shape
        q = (x @ Wq + bq).reshape(b, n, H, HD)
        k = (x @ Wk + bk).reshape(b, n, H, HD)
        v = (x @ Wv + bv).reshape(b, n, H, HD)
        scores = jnp.einsum('bqhd,bkhd->bhqk', q, k) / jnp.sqrt(jnp.float32(HD))
        scores = scores + (1.0 - adj)[None, None, :, :] * -1000000000.0
        attn = jax.nn.softmax(scores, axis=-1)
        out = jnp.einsum('bhqk,bkhd->bqhd', attn, v).reshape(b, n, d)
        return out @ Wo + bo

    def _L2_gnn_ref(x, adj, weight, bias):
        import jax, jax.numpy as jnp
        import numpy as np
        B, N, F_IN, F_OUT = (16, 1024, 256, 256)
        deg = adj.sum(axis=1)
        deg_inv_sqrt = jnp.where(deg > 0, jax.lax.rsqrt(deg), 0.0)
        norm_adj = adj * deg_inv_sqrt[:, None] * deg_inv_sqrt[None, :]
        support = jnp.einsum('bni,io->bno', x, weight)
        output = jnp.einsum('nm,bmo->bno', norm_adj, support)
        return output + bias

    def _L3_gnn_ref(x, W1, W2, b):
        import jax, jax.numpy as jnp
        import numpy as np
        A = jnp.einsum('od,bdn->bon', W1, x)
        C = jnp.einsum('od,bdn->bon', W2, x) + b[None, :, None]
        pre = A[:, :, None, :] + (C - A)[:, :, :, None]
        out = jnp.max(jax.nn.relu(pre), axis=-1)
        return out
    x = _layernorm(x + _L0_gnn_ref(x, L0_gnn_w_qkv, L0_gnn_w_proj, L0_gnn_b_proj, L0_gnn_ln_gamma, L0_gnn_ln_beta, adj), axis=-1)
    x = _layernorm(x + _L1_gnn_ref(x, adj, L1_gnn_Wq, L1_gnn_bq, L1_gnn_Wk, L1_gnn_bk, L1_gnn_Wv, L1_gnn_bv, L1_gnn_Wo, L1_gnn_bo), axis=-1)
    x = _layernorm(x + _L2_gnn_ref(x, adj, L2_gnn_weight, L2_gnn_bias), axis=-1)
    x = _layernorm(x + _L3_gnn_ref(x, adj, adj, L3_gnn_b), axis=-1)
    return x

_drawn_inputs = setup_inputs


def setup_inputs(seed=0):
    import zlib

    import numpy as np

    out = dict(_drawn_inputs(seed))
    spreads = {'L0_gnn_b_proj': (0.0, 0.1),
     'L0_gnn_ln_gamma': (1.0, 0.2),
     'L0_gnn_ln_beta': (0.0, 0.1),
     'L1_gnn_bq': (0.0, 0.47),
     'L1_gnn_bk': (0.0, 0.8),
     'L1_gnn_bv': (0.0, 0.1),
     'L1_gnn_bo': (0.0, 0.1),
     'L2_gnn_bias': (0.0, 0.1)}
    factors = {'L3_gnn_b': 8.0}
    for name, (base, spread) in spreads.items():
        noise = np.random.default_rng([zlib.crc32(name.encode()), seed]).standard_normal(out[name].shape)
        drawn = base * np.exp(spread * noise) if base else spread * noise
        out[name] = jnp.asarray(drawn.astype(out[name].dtype))
    for name, factor in factors.items():
        out[name] = (out[name] * factor).astype(out[name].dtype)
    return out
```

```python
from contextlib import ExitStack

import concourse.bass as bass
from concourse import mybir

F32 = mybir.dt.float32
F32R = mybir.dt.float32r
BF16 = mybir.dt.bfloat16
ALU = mybir.AluOpType
ACT = mybir.ActivationFunctionType
AX_X = mybir.AxisListType.X

P = 128
D = 256
FC = D // P
HEADS = 8
HD = D // HEADS
GROUPS = P // HD
NB = 2
EPS = 1e-5
ATT_SCALE = float(HD) ** -0.5
MASKED_A = -1e38
MASKED_B = 1e9

RING = [
    ("q_A", 0), ("k_A", 0), ("v_A", 0),
    ("conv", 3),
    ("pT0_B", 2), ("pT1_B", 2), ("pT2_B", 2), ("pT3_B", 2), ("o_B", 2), ("proj_B", 2),
    ("xT_B", 1), ("q_B", 1), ("k_B", 1), ("v_B", 1),
    ("mix", 2), ("pool", 3),
    ("pT0_A", 0), ("pT1_A", 0), ("pT2_A", 0), ("pT3_A", 0), ("o_A", 0), ("proj_A", 0),
    ("xT_A", -1),
]
RING_AT = {name: n for n, (name, _) in enumerate(RING)}
RING_BANKS = 4
LAST_LAG = 3
FIRST_LOOPED = LAST_LAG + 1


def gnn_kernel(nc, a, out, batches):
    pairs = batches // NB

    def has(i, lag):
        return not isinstance(i, int) or 0 <= i - lag < pairs

    def last_holder(name, i):
        at = RING_AT[name]
        back = 0
        while back < 8:
            at -= 1
            if at < 0:
                at += len(RING)
                back += 1
            if at % RING_BANKS == RING_AT[name] % RING_BANKS and has(i - back if back else i, RING[at][1]):
                if isinstance(i, int) and i - back < -1:
                    return None
                return RING[at][0], i - back - RING[at][1]
        return None

    with ExitStack() as ctx:
        def sb(name, shape, dt=F32):
            return ctx.enter_context(nc.sbuf_tensor(name, shape, dt))

        def sem(name):
            return ctx.enter_context(nc.semaphore(name))

        ident = sb("ident", [P, P])
        ident_bf = sb("ident_bf", [P, P], BF16)
        adj = sb("adj", [P, P])
        adj_T = sb("adj_T", [P, P])
        norm_adj_T = sb("norm_adj_T", [P, P])
        row_scaled = sb("row_scaled", [P, P])
        degree = sb("degree", [P, 4])
        mask = {s: sb(f"mask_{s}", [P, GROUPS, P], BF16) for s in "AB"}
        minus_half = sb("minus_half", [P, NB])
        stage = sb("stage", [P, FC, 4 * D])
        w_hi = {s: sb(f"w_hi_{s}", [P, FC, 4 * D], F32R) for s in "AB"}
        w_lo = {s: sb(f"w_lo_{s}", [P, FC, 4 * D], F32R) for s in "AB"}
        conv_hi = sb("conv_hi", [P, FC, D], F32R)
        conv_lo = sb("conv_lo", [P, FC, D], F32R)
        b_proj = sb("b_proj", [P, D])
        gamma = sb("gamma", [P, D])
        beta = sb("beta", [P, D])
        b_out = sb("b_out", [P, D])
        b_conv = sb("b_conv", [P, D])
        bq = sb("bq", [P, FC])
        bk = sb("bk", [P, FC])
        bv = sb("bv", [P, FC])
        b_pool = sb("b_pool", [P, 1])

        x_in = {s: sb(f"x_in_{s}", [P, NB, D]) for s in "ABCD"}
        resid = {s: sb(f"resid_{s}", [P, NB, D]) for s in "ABC"}
        xT_hi = {s: sb(f"xT_hi_{s}", [P, FC, NB * P], F32R) for s in "AB"}
        xT_lo = {s: sb(f"xT_lo_{s}", [P, FC, NB * P], F32R) for s in "AB"}
        qT = {s: sb(f"qT_{s}", [P, FC, NB, P]) for s in "AB"}
        kT = {s: sb(f"kT_{s}", [P, FC, NB, P]) for s in "AB"}
        v = {s: sb(f"v_{s}", [P, NB, D]) for s in "AB"}
        neg_max = {s: sb(f"neg_max_{s}", [P, GROUPS, FC * NB]) for s in "AB"}
        probs = {s: sb(f"probs_{s}", [P, NB, HEADS, P]) for s in "AB"}
        denom = {s: sb(f"denom_{s}", [P, NB, HEADS]) for s in "AB"}
        inv_denom = {s: sb(f"inv_denom_{s}", [P, NB, HEADS]) for s in "AB"}
        pT = {s: sb(f"pT_{s}", [P, NB, FC, GROUPS * P]) for s in "AB"}
        oT_hi = {s: sb(f"oT_hi_{s}", [P, FC, NB, P], F32R) for s in "AB"}
        oT_lo = {s: sb(f"oT_lo_{s}", [P, FC, NB, P], F32R) for s in "AB"}
        mixT_hi = sb("mixT_hi", [P, FC, NB, P], F32R)
        mixT_lo = sb("mixT_lo", [P, FC, NB, P], F32R)
        att_out = sb("att_out", [P, NB, D])
        centred = sb("centred", [P, NB, D])
        pre_sum = sb("pre_sum", [P, NB, D])
        z = {s: sb(f"z_{s}", [P, NB, D]) for s in "ABCD"}
        pooled = sb("pooled", [P, NB, D])
        pool_shift = sb("pool_shift", [P, NB, D])
        pool_relu = sb("pool_relu", [P, NB, D])
        pool_max = sb("pool_max", [P, NB])
        norm_of = "IABCD"
        stats = {s: sb(f"stats_{s}", [P, NB, 6]) for s in norm_of}
        mean_var = {s: sb(f"mean_var_{s}", [P, NB, 2]) for s in norm_of}
        var_eps = {s: sb(f"var_eps_{s}", [P, NB]) for s in norm_of}
        rstd = {s: sb(f"rstd_{s}", [P, NB]) for s in norm_of}
        result = sb("result", [P, NB, D])

        scores = [ctx.enter_context(nc.psum_tensor(f"scores{g}", [P, 512], F32)) for g in range(GROUPS)]
        ring = [ctx.enter_context(nc.psum_tensor(f"ring{n}", [P, 512], F32)) for n in range(RING_BANKS)]

        def bank(name):
            return ring[RING_AT[name] % RING_BANKS]

        const_loaded = sem("const_loaded")
        weights_loaded = sem("weights_loaded")
        stage_split = sem("stage_split")
        ident_zero = sem("ident_zero")
        ident_ready = sem("ident_ready")
        setup_dve = sem("setup_dve")
        setup_pow = sem("setup_pow")
        setup_pe = sem("setup_pe")
        setup_done = sem("setup_done")
        weights_hi = sem("weights_hi")
        x_loaded = sem("x_loaded")
        result_stored = sem("result_stored")
        filled = {name: sem(f"filled_{name}") for name, _ in RING}
        emptied = {name: sem(f"emptied_{name}") for name, _ in RING}
        xT_hi_ready = {s: sem(f"xT_hi_ready_{s}") for s in "AB"}
        oT_hi_ready = {s: sem(f"oT_hi_ready_{s}") for s in "AB"}
        mix_hi_ready = sem("mix_hi_ready")
        scored = {s: [sem(f"scored_{s}{g}") for g in range(GROUPS)] for s in "AB"}
        max_ready = {s: [sem(f"max_ready_{s}{g}") for g in range(GROUPS)] for s in "AB"}
        scores_read = {s: [sem(f"scores_read_{s}{g}") for g in range(GROUPS)] for s in "AB"}
        exp_ready = {s: [sem(f"exp_ready_{s}{b}") for b in range(NB)] for s in "AB"}
        inv_ready = {s: [sem(f"inv_ready_{s}{b}") for b in range(NB)] for s in "AB"}
        probs_ready = {s: [sem(f"probs_ready_{s}{b}") for b in range(NB)] for s in "AB"}
        resid_ready = {s: sem(f"resid_ready_{s}") for s in "ABC"}
        pre_sum_ready = sem("pre_sum_ready")
        centred_ready = sem("centred_ready")
        z_ready = {s: sem(f"z_ready_{s}") for s in "AD"}
        stats_ready = {s: sem(f"stats_ready_{s}") for s in norm_of}
        mean_ready = {s: sem(f"mean_ready_{s}") for s in norm_of}
        var_ready = {s: sem(f"var_ready_{s}") for s in norm_of}
        rstd_ready = {s: sem(f"rstd_ready_{s}") for s in norm_of}
        normed = {s: sem(f"normed_{s}") for s in "ABCD"}
        pool_shift_ready = sem("pool_shift_ready")
        pool_relu_ready = sem("pool_relu_ready")
        z_of = {"I": emptied["proj_A"], "A": z_ready["A"], "B": emptied["proj_B"], "C": emptied["conv"],
                "D": z_ready["D"]}
        norm_in = {"I": att_out, **z}
        norm_out = {"A": x_in["B"], "B": x_in["C"], "C": x_in["D"], "D": result}

        def row(name):
            return a[name].rearrange("(o d) -> o d", o=1).to_broadcast([P, D])

        def column(name, c):
            return a[name][c * P:(c + 1) * P].rearrange("(p o) -> p o", o=1)

        def chunked(name):
            return a[name].rearrange("(c p) n -> p c n", p=P)

        def everywhere(t):
            return t[:].rearrange("p (o d) -> p o d", o=1).to_broadcast([P, NB, D])

        x_dram = a["x"].rearrange("(n b) t d -> n t b d", b=NB)
        out_dram = out.rearrange("(n b) t d -> n t b d", b=NB)

        const_loads = [
            (adj[:], a["adj"]),
            (b_proj[:], row("L0_gnn_b_proj")), (gamma[:], row("L0_gnn_ln_gamma")),
            (beta[:], row("L0_gnn_ln_beta")), (b_out[:], row("L1_gnn_bo")), (b_conv[:], row("L2_gnn_bias")),
            (b_pool[:], column("L3_gnn_b", 0)),
        ] + [(dst[:, c:c + 1], column(name, c)) for dst, name in ((bq, "L1_gnn_bq"), (bk, "L1_gnn_bk"), (bv, "L1_gnn_bv"))
             for c in range(FC)]
        weight_sets = [
            ([(0, 3 * D, "L0_gnn_w_qkv"), (3 * D, D, "L0_gnn_w_proj")], w_hi["A"][:], w_lo["A"][:]),
            ([(0, D, "L1_gnn_Wq"), (D, D, "L1_gnn_Wk"), (2 * D, D, "L1_gnn_Wv"), (3 * D, D, "L1_gnn_Wo")],
             w_hi["B"][:], w_lo["B"][:]),
            ([(0, D, "L2_gnn_weight")], conv_hi[:], conv_lo[:]),
        ]

        def program(iteration, eng):
            for i in range(-1, FIRST_LOOPED):
                iteration(i)
            with eng.Fori(FIRST_LOOPED, pairs - 1) as i:
                iteration(i)
            for i in range(pairs - 1, pairs + LAST_LAG):
                iteration(i)

        block = ctx.enter_context(nc.Block())

        @block.sync
        def _(sp):
            for dst, src in const_loads:
                sp.dma_start(dst, src).then_inc(const_loaded, 16)
            sp.dma_start(x_in["A"][:], x_dram[0]).then_inc(x_loaded, 16)
            for n, (parts, _, _) in enumerate(weight_sets):
                if n:
                    sp.wait_ge(stage_split, n)
                for at, width, name in parts:
                    sp.dma_start(stage[:, :, at:at + width], chunked(name)).then_inc(weights_loaded, 16)

            def iteration(i):
                if has(i, -1) and not (isinstance(i, int) and i == -1):
                    sp.wait_ge(filled["xT_A"], i + 1)
                    sp.wait_ge(resid_ready["A"], i + 1)
                    sp.dma_start(x_in["A"][:], x_dram[i + 1]).then_inc(x_loaded, 16)
                if has(i, 3):
                    sp.wait_ge(normed["D"], i - 2)
                    sp.dma_start(out_dram[i - 3], result[:]).then_inc(result_stored, 16)

            program(iteration, sp)
            sp.wait_ge(result_stored, 16 * pairs)

        @block.tensor
        def _(pe):
            mm, tr = nc.tensor.matmul, nc.tensor.transpose
            pe.wait_ge(ident_ready, 1)
            pe.wait_ge(const_loaded, 16 * len(const_loads))
            tr(scores[0][:, 0:P], adj[:], ident[:])
            pe.wait_ge(setup_dve, 5)
            tr(scores[0][:, P:2 * P], row_scaled[:], ident[:]).then_inc(setup_pe, 1)
            pe.wait_ge(setup_done, 1)
            pe.wait_ge(stage_split, len(weight_sets))

            def take_bank(name, i):
                held = last_holder(name, i)
                if held:
                    pe.wait_ge(emptied[held[0]], held[1] + 1)

            def transposed_input(s, p, i):
                name = "xT_" + s
                if s == "A":
                    pe.wait_ge(x_loaded, 16 * (p + 1))
                else:
                    pe.wait_ge(normed["A"], p + 1)
                take_bank(name, i)
                for c in range(FC):
                    for b in range(NB):
                        at = (c * NB + b) * P
                        last = tr(bank(name)[:, at:at + P], x_in[s][:, b, c * P:(c + 1) * P], ident[:])
                last.then_inc(filled[name], 1)

            def qkv(s, p, i):
                pe.wait_ge(emptied["xT_" + s], p + 1)
                for part, name in enumerate(("q_" + s, "k_" + s)):
                    take_bank(name, i)
                    for oc in range(FC):
                        cols = slice(part * D + oc * P, part * D + (oc + 1) * P)
                        terms = [(w, x, c) for w, x in ((w_lo[s], xT_hi[s]), (w_hi[s], xT_lo[s]), (w_hi[s], xT_hi[s]))
                                 for c in range(FC)]
                        for n, (w, x, c) in enumerate(terms):
                            last = mm(bank(name)[:, oc * NB * P:(oc + 1) * NB * P], w[:, c, cols], x[:, c, :],
                                      start=(n == 0), stop=(n == len(terms) - 1))
                    last.then_inc(filled[name], 1)
                name = "v_" + s
                take_bank(name, i)
                for b in range(NB):
                    terms = [(x, w, c) for x, w in ((xT_lo[s], w_hi[s]), (xT_hi[s], w_lo[s]), (xT_hi[s], w_hi[s]))
                             for c in range(FC)]
                    for n, (x, w, c) in enumerate(terms):
                        last = mm(bank(name)[:, b * D:(b + 1) * D], x[:, c, b * P:(b + 1) * P],
                                  w[:, c, 2 * D:3 * D], start=(n == 0), stop=(n == len(terms) - 1))
                last.then_inc(filled[name], 1)

            def score(s, p, before):
                for g in range(GROUPS):
                    if before is not None:
                        pe.wait_ge(scores_read[before[0]][g], before[1] + 1)
                    mm(scores[g][:], ident_bf[:], mask[s][:].rearrange("p a b -> p (a b)"), start=True, stop=False)
                pe.wait_ge(emptied["q_" + s], p + 1)
                pe.wait_ge(emptied["k_" + s], p + 1)
                for c in range(FC):
                    for b in range(NB):
                        end = c == FC - 1 and b == NB - 1
                        for g in range(GROUPS):
                            at, rows = (c * NB + b) * P, slice(g * HD, (g + 1) * HD)
                            last = mm(scores[g][:, at:at + P], qT[s][rows, c, b, :], kT[s][rows, c, b, :],
                                      start=False, stop=end)
                            if end:
                                last.then_inc(scored[s][g], 1)

            def probs_transpose(s, p, i, n):
                b, c = divmod(n, FC)
                name = f"pT{n}_{s}"
                pe.wait_ge(probs_ready[s][b], p + 1)
                take_bank(name, i)
                for g in range(GROUPS):
                    last = tr(bank(name)[:, g * P:(g + 1) * P], probs[s][:, b, c * GROUPS + g, :], ident[:])
                last.then_inc(filled[name], 1)

            def values(s, p, i, b):
                name = "o_" + s
                if b == 0:
                    take_bank(name, i)
                    pe.wait_ge(emptied["v_" + s], p + 1)
                for c in range(FC):
                    pe.wait_ge(emptied[f"pT{b * FC + c}_{s}"], p + 1)
                    for g in range(GROUPS):
                        h, at = c * GROUPS + g, (c * NB + b) * P
                        last = mm(bank(name)[g * HD:(g + 1) * HD, at:at + P], v[s][:, b, h * HD:(h + 1) * HD],
                                  pT[s][:, b, c, g * P:(g + 1) * P], start=True, stop=True)
                if b == NB - 1:
                    last.then_inc(filled[name], 1)

            def by_features(name, s, i, hi, lo, w_hi_, w_lo_):
                take_bank(name, i)
                for b in range(NB):
                    terms = [(x, w, c) for x, w in ((hi, w_lo_), (lo, w_hi_), (hi, w_hi_)) for c in range(FC)]
                    for n, (x, w, c) in enumerate(terms):
                        last = mm(bank(name)[:, b * D:(b + 1) * D], x[:, c, b, :], w[:, c, :],
                                  start=(n == 0), stop=(n == len(terms) - 1))
                last.then_inc(filled[name], 1)

            def attention_output(s, p, i):
                probs_transpose(s, p, i, 0)
                probs_transpose(s, p, i, 1)
                probs_transpose(s, p, i, 2)
                probs_transpose(s, p, i, 3)
                values(s, p, i, 0)
                values(s, p, i, 1)
                pe.wait_ge(emptied["o_" + s], p + 1)
                by_features("proj_" + s, s, i, oT_hi[s], oT_lo[s], w_hi[s][:, :, 3 * D:], w_lo[s][:, :, 3 * D:])

            def iteration(i):
                if has(i, 0):
                    qkv("A", i, i)
                if has(i, 3):
                    pe.wait_ge(emptied["mix"], i - 2)
                    by_features("conv", "C", i, mixT_hi, mixT_lo, conv_hi[:], conv_lo[:])
                if has(i, 2):
                    attention_output("B", i - 2, i)
                if has(i, 1):
                    transposed_input("B", i - 1, i)
                if has(i, 0):
                    score("A", i, ("B", i - 2) if has(i, 2) else ("A", i - 1) if has(i, 1) else None)
                if has(i, 1):
                    qkv("B", i - 1, i)
                if has(i, 2):
                    pe.wait_ge(normed["B"], i - 1)
                    take_bank("mix", i)
                    for c in range(FC):
                        for b in range(NB):
                            at = (c * NB + b) * P
                            last = mm(bank("mix")[:, at:at + P], x_in["C"][:, b, c * P:(c + 1) * P], norm_adj_T[:],
                                      start=True, stop=True)
                    last.then_inc(filled["mix"], 1)
                if has(i, 3):
                    pe.wait_ge(normed["C"], i - 2)
                    take_bank("pool", i)
                    mm(bank("pool")[:], adj_T[:], x_in["D"][:].rearrange("p b d -> p (b d)"),
                       start=True, stop=True).then_inc(filled["pool"], 1)
                if has(i, 0):
                    attention_output("A", i, i)
                if has(i, -1):
                    transposed_input("A", i + 1, i)
                if has(i, 1):
                    score("B", i - 1, ("A", i) if has(i, 0) else ("B", i - 2))

            program(iteration, pe)

        @block.scalar
        def _(act):
            seen = 0
            for n, (parts, hi, _) in enumerate(weight_sets):
                seen += len(parts)
                act.wait_ge(weights_loaded, 16 * seen)
                nc.scalar.copy(hi, stage[:, :, 0:hi.shape[2]]).then_inc(weights_hi, 1)
            act.wait_ge(const_loaded, 16 * len(const_loads))

            def input_hi(s, p):
                act.wait_ge(filled["xT_" + s], p + 1)
                nc.scalar.copy(xT_hi[s][:].rearrange("p c t -> p (c t)"), bank("xT_" + s)[:]).then_inc(xT_hi_ready[s], 1)

            def save_v(s, p):
                act.wait_ge(filled["v_" + s], p + 1)
                nc.scalar.copy(v[s][:].rearrange("p b d -> p (b d)"), bank("v_" + s)[:]).then_inc(emptied["v_" + s], 1)

            def exps(s, p, b):
                for g in range(GROUPS):
                    if b == 0:
                        act.wait_ge(max_ready[s][g], p + 1)
                    for c in range(FC):
                        h, slot = c * GROUPS + g, c * NB + b
                        last = nc.scalar.activation(probs[s][:, b, h, :], scores[g][:, slot * P:(slot + 1) * P], ACT.Exp,
                                                    bias=neg_max[s][:, g, slot:slot + 1],
                                                    accum_out=denom[s][:, b, h:h + 1])
                    if b == NB - 1:
                        last.then_inc(scores_read[s][g], 1)
                if b < NB - 1:
                    last.then_inc(exp_ready[s][b], 1)

            def save_probs(s, p, n):
                name = f"pT{n}_{s}"
                act.wait_ge(filled[name], p + 1)
                nc.scalar.copy(pT[s][:, n // FC, n % FC, :], bank(name)[:]).then_inc(emptied[name], 1)

            def heads_hi(s, p):
                act.wait_ge(filled["o_" + s], p + 1)
                for c in range(FC):
                    cols = slice(c * NB * P, (c + 1) * NB * P)
                    dst = oT_hi[s][:, c].rearrange("p b t -> p (b t)")
                    if s == "A":
                        last = nc.scalar.copy(dst, bank("o_A")[:, cols])
                    else:
                        last = nc.scalar.activation(dst, bank("o_B")[:, cols], ACT.Identity, bias=bv[:, c:c + 1])
                last.then_inc(oT_hi_ready[s], 1)

            def iteration(i):
                if has(i, 2):
                    exps("B", i - 2, 0)
                if has(i, 0):
                    save_v("A", i)
                if has(i, 2):
                    exps("B", i - 2, 1)
                    for n in range(NB * FC):
                        save_probs("B", i - 2, n)
                    heads_hi("B", i - 2)
                if has(i, 1):
                    input_hi("B", i - 1)
                if has(i, 0):
                    exps("A", i, 0)
                if has(i, 1):
                    save_v("B", i - 1)
                if has(i, 0):
                    exps("A", i, 1)
                if has(i, 2):
                    act.wait_ge(filled["mix"], i - 1)
                    nc.scalar.copy(mixT_hi[:].rearrange("p c b t -> p (c b t)"), bank("mix")[:]).then_inc(mix_hi_ready, 1)
                if has(i, 3):
                    act.wait_ge(filled["pool"], i - 2)
                    nc.scalar.copy(pooled[:].rearrange("p b d -> p (b d)"), bank("pool")[:]).then_inc(emptied["pool"], 1)
                if has(i, 0):
                    for n in range(NB * FC):
                        save_probs("A", i, n)
                    heads_hi("A", i)
                if has(i, -1):
                    input_hi("A", i + 1)

            program(iteration, act)

        @block.vector
        def _(dve):
            tt, ts, stt = nc.vector.tensor_tensor, nc.vector.tensor_scalar, nc.vector.scalar_tensor_tensor
            dve.wait_ge(const_loaded, 16 * len(const_loads))
            adj_4 = adj[:].rearrange("p (o d) -> p o d", o=1).to_broadcast([P, GROUPS, P])
            ts(mask["A"][:], adj_4, 0.0, MASKED_A, ALU.is_equal, ALU.mult)
            ts(mask["B"][:], adj_4, 1.0, MASKED_B, ALU.subtract, ALU.mult)
            nc.vector.tensor_reduce(degree[:, 0:1], adj[:], AX_X, ALU.add).then_inc(setup_dve, 1)
            dve.wait_ge(setup_dve, 1)
            ts(degree[:, 1:2], degree[:, 0:1], 1e-30, None, ALU.max).then_inc(setup_dve, 1)
            ts(degree[:, 2:3], degree[:, 0:1], 0.0, None, ALU.is_gt).then_inc(setup_dve, 1)
            dve.wait_ge(setup_dve, 3)
            dve.wait_ge(setup_pow, 1)
            tt(degree[:, 0:1], degree[:, 3:4], degree[:, 2:3], ALU.mult).then_inc(setup_dve, 1)
            dve.wait_ge(setup_dve, 4)
            ts(row_scaled[:], adj[:], degree[:, 0:1], None, ALU.mult).then_inc(setup_dve, 1)
            dve.wait_ge(ident_ready, 1)
            nc.vector.tensor_copy(ident_bf[:], ident[:])
            dve.wait_ge(setup_pe, 1)
            nc.vector.tensor_copy(adj_T[:], scores[0][:, 0:P])
            ts(norm_adj_T[:], scores[0][:, P:2 * P], degree[:, 0:1], None, ALU.mult).then_inc(setup_done, 1)
            for n, (parts, hi, lo) in enumerate(weight_sets):
                dve.wait_ge(weights_hi, n + 1)
                tt(lo, stage[:, :, 0:lo.shape[2]], hi.bitcast(F32), ALU.subtract).then_inc(stage_split, 1)

            def input_lo(s, p):
                dve.wait_ge(xT_hi_ready[s], p + 1)
                tt(xT_lo[s][:].rearrange("p c t -> p (c t)"), bank("xT_" + s)[:],
                   xT_hi[s][:].rearrange("p c t -> p (c t)").bitcast(F32), ALU.subtract).then_inc(emptied["xT_" + s], 1)

            def row_max(s, p):
                for g in range(GROUPS):
                    dve.wait_ge(scored[s][g], p + 1)
                    nc.vector.tensor_reduce(neg_max[s][:, g, :], scores[g][:].rearrange("p (n k) -> p n k", k=P), AX_X,
                                            ALU.max, negate=True).then_inc(max_ready[s][g], 1)

            def save_qk(s, p):
                dve.wait_ge(filled["q_" + s], p + 1)
                if s == "A":
                    ts(qT[s][:].rearrange("p c b t -> p (c b t)"), bank("q_A")[:], ATT_SCALE, None,
                       ALU.mult).then_inc(emptied["q_A"], 1)
                    dve.wait_ge(filled["k_A"], p + 1)
                    nc.vector.tensor_copy(kT[s][:].rearrange("p c b t -> p (c b t)"), bank("k_A")[:]).then_inc(emptied["k_A"], 1)
                    return
                for c in range(FC):
                    last = ts(qT[s][:, c].rearrange("p b t -> p (b t)"), bank("q_B")[:, c * NB * P:(c + 1) * NB * P],
                              bq[:, c:c + 1], ATT_SCALE, ALU.add, ALU.mult)
                last.then_inc(emptied["q_B"], 1)
                dve.wait_ge(filled["k_B"], p + 1)
                for c in range(FC):
                    last = ts(kT[s][:, c].rearrange("p b t -> p (b t)"), bank("k_B")[:, c * NB * P:(c + 1) * NB * P],
                              bk[:, c:c + 1], None, ALU.add)
                last.then_inc(emptied["k_B"], 1)

            def invert(s, p, b):
                if b < NB - 1:
                    dve.wait_ge(exp_ready[s][b], p + 1)
                else:
                    dve.wait_ge(scores_read[s][GROUPS - 1], p + 1)
                nc.vector.reciprocal(inv_denom[s][:, b, :], denom[s][:, b, :]).then_inc(inv_ready[s][b], 1)

            def heads_lo(s, p):
                dve.wait_ge(oT_hi_ready[s], p + 1)
                if s == "A":
                    tt(oT_lo[s][:].rearrange("p c b t -> p (c b t)"), bank("o_A")[:],
                       oT_hi[s][:].rearrange("p c b t -> p (c b t)").bitcast(F32), ALU.subtract).then_inc(emptied["o_A"], 1)
                    return
                for c in range(FC):
                    last = stt(out=oT_lo[s][:, c].rearrange("p b t -> p (b t)"),
                               in0=bank("o_B")[:, c * NB * P:(c + 1) * NB * P], scalar=bv[:, c:c + 1],
                               in1=oT_hi[s][:, c].rearrange("p b t -> p (b t)").bitcast(F32),
                               op0=ALU.add, op1=ALU.subtract)
                last.then_inc(emptied["o_B"], 1)

            def statistics(s, p):
                dve.wait_ge(z_of[s], p + 1)
                for b in range(NB):
                    last = nc.vector.bn_stats(stats[s][:, b, :], norm_in[s][:, b, :])
                last.then_inc(stats_ready[s], 1)
                dve.wait_ge(setup_done, 1)
                dve.wait_ge(stats_ready[s], p + 1)
                for b in range(NB):
                    last = nc.vector.bn_aggr(mean_var[s][:, b, :], stats[s][:, b, :])
                last.then_inc(mean_ready[s], 1)
                dve.wait_ge(mean_ready[s], p + 1)
                ts(var_eps[s][:], mean_var[s][:, :, 1], EPS, None, ALU.add).then_inc(var_ready[s], 1)

            def normalise(s, p, taken):
                dve.wait_ge(rstd_ready[s], p + 1)
                for sem_, value in taken:
                    dve.wait_ge(sem_, value)
                for b in range(NB):
                    last = ts(norm_out[s][:, b, :], norm_in[s][:, b, :], mean_var[s][:, b, 0:1], rstd[s][:, b:b + 1],
                              ALU.subtract, ALU.mult)
                last.then_inc(normed[s], 1)

            def add_resid(s, p, name):
                dve.wait_ge(filled[name], p + 1)
                dve.wait_ge(resid_ready[s], p + 1)
                tt(z[s][:].rearrange("p b d -> p (b d)"), bank(name)[:], resid[s][:].rearrange("p b d -> p (b d)"),
                   ALU.add).then_inc(emptied[name], 1)

            def before(sem_, p, one=1):
                return [] if isinstance(p, int) and p == 0 else [(sem_, p * one)]

            def iteration(i):
                if has(i, 0):
                    save_qk("A", i)
                if has(i, 2):
                    invert("B", i - 2, 0)
                if has(i, 3):
                    add_resid("C", i - 3, "conv")
                    statistics("C", i - 3)
                if has(i, 2):
                    invert("B", i - 2, 1)
                if has(i, 3):
                    normalise("C", i - 3, before(filled["pool"], i - 3) + before(z_ready["D"], i - 3))
                if has(i, 2):
                    heads_lo("B", i - 2)
                    add_resid("B", i - 2, "proj_B")
                    statistics("B", i - 2)
                if has(i, 1):
                    input_lo("B", i - 1)
                if has(i, 2):
                    normalise("B", i - 2, before(filled["mix"], i - 2) + before(resid_ready["C"], i - 2))
                if has(i, 0):
                    row_max("A", i)
                if has(i, 1):
                    save_qk("B", i - 1)
                if has(i, 0):
                    invert("A", i, 0)
                if has(i, 3):
                    dve.wait_ge(emptied["pool"], i - 2)
                    nc.vector.tensor_reduce(pool_max[:], pooled[:], AX_X, ALU.max)
                    stt(out=pool_shift[:].rearrange("p b d -> p (b d)"), in0=pooled[:].rearrange("p b d -> p (b d)"),
                        scalar=b_pool[:, 0:1], in1=pooled[:].rearrange("p b d -> p (b d)"),
                        op0=ALU.add, op1=ALU.subtract).then_inc(pool_shift_ready, 1)
                    dve.wait_ge(pool_shift_ready, i - 2)
                    for b in range(NB):
                        last = ts(pool_relu[:, b, :], pool_shift[:, b, :], pool_max[:, b:b + 1], 0.0, ALU.add, ALU.max)
                    last.then_inc(pool_relu_ready, 1)
                    dve.wait_ge(pool_relu_ready, i - 2)
                    tt(z["D"][:], pool_relu[:], x_in["D"][:], ALU.add).then_inc(z_ready["D"], 1)
                    statistics("D", i - 3)
                if has(i, 2):
                    dve.wait_ge(mix_hi_ready, i - 1)
                    tt(mixT_lo[:].rearrange("p c b t -> p (c b t)"), bank("mix")[:],
                       mixT_hi[:].rearrange("p c b t -> p (c b t)").bitcast(F32), ALU.subtract).then_inc(emptied["mix"], 1)
                if has(i, 0):
                    invert("A", i, 1)
                if has(i, 3):
                    normalise("D", i - 3, before(result_stored, i - 3, 16))
                if has(i, 0):
                    heads_lo("A", i)
                    dve.wait_ge(filled["proj_A"], i + 1)
                    tt(att_out[:], bank("proj_A")[:].rearrange("p (b d) -> p b d", b=NB), everywhere(b_proj),
                       ALU.add).then_inc(emptied["proj_A"], 1)
                    statistics("I", i)
                if has(i, -1):
                    input_lo("A", i + 1)
                if has(i, 0):
                    for b in range(NB):
                        last = stt(out=centred[:, b, :], in0=att_out[:, b, :], scalar=mean_var["I"][:, b, 0:1],
                                   in1=gamma[:], op0=ALU.subtract, op1=ALU.mult)
                    last.then_inc(centred_ready, 1)
                    dve.wait_ge(centred_ready, i + 1)
                    dve.wait_ge(rstd_ready["I"], i + 1)
                    dve.wait_ge(pre_sum_ready, i + 1)
                    for b in range(NB):
                        last = stt(out=z["A"][:, b, :], in0=centred[:, b, :], scalar=rstd["I"][:, b:b + 1],
                                   in1=pre_sum[:, b, :], op0=ALU.mult, op1=ALU.add)
                    last.then_inc(z_ready["A"], 1)
                    statistics("A", i)
                if has(i, 1):
                    row_max("B", i - 1)
                if has(i, 0):
                    normalise("A", i, before(filled["xT_B"], i) + before(resid_ready["B"], i))

            program(iteration, dve)

        @block.gpsimd
        def _(pool):
            tt = nc.gpsimd.tensor_tensor
            nc.gpsimd.memset(minus_half[:], -0.5)
            nc.gpsimd.memset(ident[:], 0.0).then_inc(ident_zero, 1)
            pool.wait_ge(ident_zero, 1)
            nc.gpsimd.affine_select(out=ident[:], in_=ident[:], compare_op=ALU.not_equal, fill=1.0, base=0,
                                    pattern=[[-1, P]], channel_multiplier=1).then_inc(ident_ready, 1)
            pool.wait_ge(const_loaded, 16 * len(const_loads))
            pool.wait_ge(ident_ready, 1)
            pool.wait_ge(setup_dve, 3)
            tt(degree[:, 3:4], degree[:, 1:2], minus_half[:, 0:1], ALU.pow).then_inc(setup_pow, 1)

            def residual(s, p, ready, value, bias):
                pool.wait_ge(ready, value)
                if s != "A" and not (isinstance(p, int) and p == 0):
                    pool.wait_ge(emptied["proj_B" if s == "B" else "conv"], p)
                if s == "A" and not (isinstance(p, int) and p == 0):
                    pool.wait_ge(pre_sum_ready, p)
                tt(resid[s][:], x_in[s][:], everywhere(bias), ALU.add).then_inc(resid_ready[s], 1)

            def scale_probs(s, p, b):
                pool.wait_ge(inv_ready[s][b], p + 1)
                tt(probs[s][:, b], probs[s][:, b],
                   inv_denom[s][:, b, :].rearrange("p (h o) -> p h o", o=1).to_broadcast([P, HEADS, P]),
                   ALU.mult).then_inc(probs_ready[s][b], 1)

            def inverse_root(s, p):
                pool.wait_ge(var_ready[s], p + 1)
                tt(rstd[s][:], var_eps[s][:], minus_half[:], ALU.pow).then_inc(rstd_ready[s], 1)

            def iteration(i):
                if has(i, 0):
                    residual("A", i, x_loaded, 16 * (i + 1), beta)
                if has(i, 2):
                    scale_probs("B", i - 2, 0)
                if has(i, 3):
                    inverse_root("C", i - 3)
                if has(i, 2):
                    scale_probs("B", i - 2, 1)
                if has(i, 1):
                    residual("B", i - 1, normed["A"], i, b_out)
                if has(i, 2):
                    inverse_root("B", i - 2)
                    residual("C", i - 2, normed["B"], i - 1, b_conv)
                if has(i, 0):
                    scale_probs("A", i, 0)
                if has(i, 3):
                    inverse_root("D", i - 3)
                if has(i, 0):
                    scale_probs("A", i, 1)
                    pool.wait_ge(emptied["proj_A"], i + 1)
                    if not (isinstance(i, int) and i == 0):
                        pool.wait_ge(z_ready["A"], i)
                    pool.wait_ge(resid_ready["A"], i + 1)
                    inverse_root("I", i)
                    tt(pre_sum[:], att_out[:], resid["A"][:], ALU.add).then_inc(pre_sum_ready, 1)
                    inverse_root("A", i)

            program(iteration, pool)


_NAMES = ["x", "adj", "L0_gnn_w_qkv", "L0_gnn_w_proj", "L0_gnn_b_proj", "L0_gnn_ln_gamma", "L0_gnn_ln_beta",
          "L1_gnn_Wq", "L1_gnn_bq", "L1_gnn_Wk", "L1_gnn_bk", "L1_gnn_Wv", "L1_gnn_bv", "L1_gnn_Wo", "L1_gnn_bo",
          "L2_gnn_weight", "L2_gnn_bias", "L3_gnn_b"]


def kernel(**inputs):
    import numpy as np
    import concourse.bacc as bacc
    from concourse.bass_utils import run_bass_kernel_spmd

    nc = bacc.Bacc("TRN2", target_bir_lowering=False, num_devices=1)
    arrays, args = {}, {}
    for name in _NAMES:
        arr = np.ascontiguousarray(inputs[name])
        arrays[f"in_{name}"] = arr
        args[name] = nc.dram_tensor(f"in_{name}", arr.shape, mybir.dt.from_np(arr.dtype), kind="ExternalInput").ap()
    shape = arrays["in_x"].shape
    out = nc.dram_tensor("out", shape, F32, kind="ExternalOutput").ap()
    gnn_kernel(nc, args, out, shape[0])
    return run_bass_kernel_spmd(nc, [arrays], core_ids=[0]).results[0]["out"]
```

```python
from contextlib import ExitStack

import concourse.bass as bass
from concourse import mybir

F32 = mybir.dt.float32
F32R = mybir.dt.float32r
BF16 = mybir.dt.bfloat16
ALU = mybir.AluOpType
ACT = mybir.ActivationFunctionType
AX_X = mybir.AxisListType.X

P = 128
D = 256
FC = D // P
HEADS = 8
HD = D // HEADS
GROUPS = P // HD
NB = 2
EPS = 1e-5
ATT_SCALE = float(HD) ** -0.5
MASKED_A = -1e38
MASKED_B = 1e9

RING = [
    ("q_A", 0), ("k_A", 0), ("v_A", 0),
    ("pT0_B", 2), ("pT1_B", 2), ("pT2_B", 2), ("pT3_B", 2), ("o_B", 2),
    ("xT_B", 1), ("conv", 3), ("proj_B", 2),
    ("q_B", 1), ("k_B", 1), ("v_B", 1),
    ("pT0_A", 0), ("pT1_A", 0), ("mix", 2), ("pT2_A", 0), ("pT3_A", 0), ("o_A", 0),
    ("xT_A", -1), ("pool", 3), ("proj_A", 0),
]
RING_AT = {name: n for n, (name, _) in enumerate(RING)}
RING_BANKS = 4
LAST_LAG = 4
FIRST_LOOPED = LAST_LAG + 1


def gnn_kernel(nc, a, out, batches):
    pairs = batches // NB

    def has(i, lag):
        return not isinstance(i, int) or 0 <= i - lag < pairs

    def last_holder(name, i):
        at = RING_AT[name]
        back = 0
        while back < 8:
            at -= 1
            if at < 0:
                at += len(RING)
                back += 1
            if at % RING_BANKS == RING_AT[name] % RING_BANKS and has(i - back if back else i, RING[at][1]):
                if isinstance(i, int) and i - back < -1:
                    return None
                return RING[at][0], i - back - RING[at][1]
        return None

    with ExitStack() as ctx:
        def sb(name, shape, dt=F32):
            return ctx.enter_context(nc.sbuf_tensor(name, shape, dt))

        def sem(name):
            return ctx.enter_context(nc.semaphore(name))

        ident = sb("ident", [P, P])
        ident_bf = sb("ident_bf", [P, P], BF16)
        adj = sb("adj", [P, P])
        adj_T = sb("adj_T", [P, P])
        norm_adj_T = sb("norm_adj_T", [P, P])
        row_scaled = sb("row_scaled", [P, P])
        degree = sb("degree", [P, 4])
        mask = {s: sb(f"mask_{s}", [P, GROUPS, P], BF16) for s in "AB"}
        minus_half = sb("minus_half", [P, NB])
        stage = sb("stage", [P, FC, 4 * D])
        w_hi = {s: sb(f"w_hi_{s}", [P, FC, 4 * D], F32R) for s in "AB"}
        w_lo = {s: sb(f"w_lo_{s}", [P, FC, 4 * D], F32R) for s in "AB"}
        conv_hi = sb("conv_hi", [P, FC, D], F32R)
        conv_lo = sb("conv_lo", [P, FC, D], F32R)
        b_proj = sb("b_proj", [P, D])
        gamma = sb("gamma", [P, D])
        beta = sb("beta", [P, D])
        b_out = sb("b_out", [P, D])
        b_conv = sb("b_conv", [P, D])
        bq = sb("bq", [P, FC])
        bk = sb("bk", [P, FC])
        bv = sb("bv", [P, FC])
        b_pool = sb("b_pool", [P, 1])

        x_in = {s: sb(f"x_in_{s}", [P, NB, D]) for s in "ABCD"}
        resid = {s: sb(f"resid_{s}", [P, NB, D]) for s in "ABC"}
        xT_hi = {s: sb(f"xT_hi_{s}", [P, FC, NB * P], F32R) for s in "AB"}
        xT_lo = {s: sb(f"xT_lo_{s}", [P, FC, NB * P], F32R) for s in "AB"}
        qT = {s: sb(f"qT_{s}", [P, FC, NB, P]) for s in "AB"}
        kT = {s: sb(f"kT_{s}", [P, FC, NB, P]) for s in "AB"}
        v = {s: sb(f"v_{s}", [P, NB, D]) for s in "AB"}
        neg_max = {s: sb(f"neg_max_{s}", [P, GROUPS, FC * NB]) for s in "AB"}
        probs = {s: sb(f"probs_{s}", [P, NB, HEADS, P]) for s in "AB"}
        denom = {s: sb(f"denom_{s}", [P, NB, HEADS]) for s in "AB"}
        inv_denom = {s: sb(f"inv_denom_{s}", [P, NB, HEADS]) for s in "AB"}
        pT = {s: sb(f"pT_{s}", [P, NB, FC, GROUPS * P]) for s in "AB"}
        oT_hi = {s: sb(f"oT_hi_{s}", [P, FC, NB, P], F32R) for s in "AB"}
        oT_lo = {s: sb(f"oT_lo_{s}", [P, FC, NB, P], F32R) for s in "AB"}
        mixT_hi = sb("mixT_hi", [P, FC, NB, P], F32R)
        mixT_lo = sb("mixT_lo", [P, FC, NB, P], F32R)
        att_out = sb("att_out", [P, NB, D])
        centred = sb("centred", [P, NB, D])
        pre_sum = sb("pre_sum", [P, NB, D])
        z = {s: sb(f"z_{s}", [P, NB, D]) for s in "ABCD"}
        pooled = sb("pooled", [P, NB, D])
        pool_shift = sb("pool_shift", [P, NB, D])
        pool_relu = sb("pool_relu", [P, NB, D])
        pool_max = sb("pool_max", [P, NB])
        norm_of = "IABCD"
        stats = {s: sb(f"stats_{s}", [P, NB, 6]) for s in norm_of}
        mean_var = {s: sb(f"mean_var_{s}", [P, NB, 2]) for s in norm_of}
        var_eps = {s: sb(f"var_eps_{s}", [P, NB]) for s in norm_of}
        rstd = {s: sb(f"rstd_{s}", [P, NB]) for s in norm_of}
        result = sb("result", [P, NB, D])

        scores = [ctx.enter_context(nc.psum_tensor(f"scores{g}", [P, 512], F32)) for g in range(GROUPS)]
        ring = [ctx.enter_context(nc.psum_tensor(f"ring{n}", [P, 512], F32)) for n in range(RING_BANKS)]

        def bank(name):
            return ring[RING_AT[name] % RING_BANKS]

        const_loaded = sem("const_loaded")
        weights_loaded = sem("weights_loaded")
        stage_split = sem("stage_split")
        ident_zero = sem("ident_zero")
        ident_ready = sem("ident_ready")
        setup_dve = sem("setup_dve")
        setup_pow = sem("setup_pow")
        setup_pe = sem("setup_pe")
        setup_done = sem("setup_done")
        weights_hi = sem("weights_hi")
        x_loaded = sem("x_loaded")
        result_stored = sem("result_stored")
        filled = {name: sem(f"filled_{name}") for name, _ in RING}
        emptied = {name: sem(f"emptied_{name}") for name, _ in RING}
        xT_hi_ready = {s: sem(f"xT_hi_ready_{s}") for s in "AB"}
        oT_hi_ready = {s: sem(f"oT_hi_ready_{s}") for s in "AB"}
        mix_hi_ready = sem("mix_hi_ready")
        scored = {s: [sem(f"scored_{s}{g}") for g in range(GROUPS)] for s in "AB"}
        max_ready = {s: [sem(f"max_ready_{s}{g}") for g in range(GROUPS)] for s in "AB"}
        scores_read = {s: [sem(f"scores_read_{s}{g}") for g in range(GROUPS)] for s in "AB"}
        exp_ready = {s: [sem(f"exp_ready_{s}{b}") for b in range(NB)] for s in "AB"}
        inv_ready = {s: [sem(f"inv_ready_{s}{b}") for b in range(NB)] for s in "AB"}
        probs_ready = {s: [sem(f"probs_ready_{s}{b}") for b in range(NB)] for s in "AB"}
        resid_ready = {s: sem(f"resid_ready_{s}") for s in "ABC"}
        pre_sum_ready = sem("pre_sum_ready")
        centred_ready = sem("centred_ready")
        z_ready = {s: sem(f"z_ready_{s}") for s in "AD"}
        stats_ready = {s: sem(f"stats_ready_{s}") for s in norm_of}
        mean_ready = {s: sem(f"mean_ready_{s}") for s in norm_of}
        var_ready = {s: sem(f"var_ready_{s}") for s in norm_of}
        rstd_ready = {s: sem(f"rstd_ready_{s}") for s in norm_of}
        normed = {s: sem(f"normed_{s}") for s in "ABCD"}
        pool_shift_ready = sem("pool_shift_ready")
        pool_relu_ready = sem("pool_relu_ready")
        z_of = {"I": emptied["proj_A"], "A": z_ready["A"], "B": emptied["proj_B"], "C": emptied["conv"],
                "D": z_ready["D"]}
        norm_in = {"I": att_out, **z}
        norm_out = {"A": x_in["B"], "B": x_in["C"], "C": x_in["D"], "D": result}

        def row(name):
            return a[name].rearrange("(o d) -> o d", o=1).to_broadcast([P, D])

        def column(name, c):
            return a[name][c * P:(c + 1) * P].rearrange("(p o) -> p o", o=1)

        def chunked(name):
            return a[name].rearrange("(c p) n -> p c n", p=P)

        def everywhere(t):
            return t[:].rearrange("p (o d) -> p o d", o=1).to_broadcast([P, NB, D])

        x_dram = a["x"].rearrange("(n b) t d -> n t b d", b=NB)
        out_dram = out.rearrange("(n b) t d -> n t b d", b=NB)

        const_loads = [
            (adj[:], a["adj"]),
            (b_proj[:], row("L0_gnn_b_proj")), (gamma[:], row("L0_gnn_ln_gamma")),
            (beta[:], row("L0_gnn_ln_beta")), (b_out[:], row("L1_gnn_bo")), (b_conv[:], row("L2_gnn_bias")),
            (b_pool[:], column("L3_gnn_b", 0)),
        ] + [(dst[:, c:c + 1], column(name, c)) for dst, name in ((bq, "L1_gnn_bq"), (bk, "L1_gnn_bk"), (bv, "L1_gnn_bv"))
             for c in range(FC)]
        weight_sets = [
            ([(0, 3 * D, "L0_gnn_w_qkv"), (3 * D, D, "L0_gnn_w_proj")], w_hi["A"][:], w_lo["A"][:]),
            ([(0, D, "L1_gnn_Wq"), (D, D, "L1_gnn_Wk"), (2 * D, D, "L1_gnn_Wv"), (3 * D, D, "L1_gnn_Wo")],
             w_hi["B"][:], w_lo["B"][:]),
            ([(0, D, "L2_gnn_weight")], conv_hi[:], conv_lo[:]),
        ]

        def program(iteration, eng):
            for i in range(-1, FIRST_LOOPED):
                iteration(i)
            with eng.Fori(FIRST_LOOPED, pairs - 1) as i:
                iteration(i)
            for i in range(pairs - 1, pairs + LAST_LAG):
                iteration(i)

        block = ctx.enter_context(nc.Block())

        @block.sync
        def _(sp):
            for dst, src in const_loads:
                sp.dma_start(dst, src).then_inc(const_loaded, 16)
            sp.dma_start(x_in["A"][:], x_dram[0]).then_inc(x_loaded, 16)
            for n, (parts, _, _) in enumerate(weight_sets):
                if n:
                    sp.wait_ge(stage_split, n)
                for at, width, name in parts:
                    sp.dma_start(stage[:, :, at:at + width], chunked(name)).then_inc(weights_loaded, 16)

            def iteration(i):
                if has(i, -1) and not (isinstance(i, int) and i == -1):
                    sp.wait_ge(filled["xT_A"], i + 1)
                    sp.wait_ge(resid_ready["A"], i + 1)
                    sp.dma_start(x_in["A"][:], x_dram[i + 1]).then_inc(x_loaded, 16)
                if has(i, 4):
                    sp.wait_ge(normed["D"], i - 3)
                    sp.dma_start(out_dram[i - 4], result[:]).then_inc(result_stored, 16)

            program(iteration, sp)
            sp.wait_ge(result_stored, 16 * pairs)

        @block.tensor
        def _(pe):
            mm, tr = nc.tensor.matmul, nc.tensor.transpose
            pe.wait_ge(ident_ready, 1)
            pe.wait_ge(const_loaded, 16 * len(const_loads))
            tr(scores[0][:, 0:P], adj[:], ident[:])
            pe.wait_ge(setup_dve, 5)
            tr(scores[0][:, P:2 * P], row_scaled[:], ident[:]).then_inc(setup_pe, 1)
            pe.wait_ge(setup_done, 1)
            pe.wait_ge(stage_split, len(weight_sets))

            def take_bank(name, i):
                held = last_holder(name, i)
                if held:
                    pe.wait_ge(emptied[held[0]], held[1] + 1)

            def transposed_input(s, p, i):
                name = "xT_" + s
                if s == "A":
                    pe.wait_ge(x_loaded, 16 * (p + 1))
                else:
                    pe.wait_ge(normed["A"], p + 1)
                take_bank(name, i)
                for c in range(FC):
                    for b in range(NB):
                        at = (c * NB + b) * P
                        last = tr(bank(name)[:, at:at + P], x_in[s][:, b, c * P:(c + 1) * P], ident[:])
                last.then_inc(filled[name], 1)

            def qkv(s, p, i):
                pe.wait_ge(emptied["xT_" + s], p + 1)
                for part, name in enumerate(("q_" + s, "k_" + s)):
                    take_bank(name, i)
                    for oc in range(FC):
                        cols = slice(part * D + oc * P, part * D + (oc + 1) * P)
                        terms = [(w, x, c) for w, x in ((w_lo[s], xT_hi[s]), (w_hi[s], xT_lo[s]), (w_hi[s], xT_hi[s]))
                                 for c in range(FC)]
                        for n, (w, x, c) in enumerate(terms):
                            last = mm(bank(name)[:, oc * NB * P:(oc + 1) * NB * P], w[:, c, cols], x[:, c, :],
                                      start=(n == 0), stop=(n == len(terms) - 1))
                    last.then_inc(filled[name], 1)
                name = "v_" + s
                take_bank(name, i)
                for b in range(NB):
                    terms = [(x, w, c) for x, w in ((xT_lo[s], w_hi[s]), (xT_hi[s], w_lo[s]), (xT_hi[s], w_hi[s]))
                             for c in range(FC)]
                    for n, (x, w, c) in enumerate(terms):
                        last = mm(bank(name)[:, b * D:(b + 1) * D], x[:, c, b * P:(b + 1) * P],
                                  w[:, c, 2 * D:3 * D], start=(n == 0), stop=(n == len(terms) - 1))
                last.then_inc(filled[name], 1)

            def score_mask(s, before):
                for g in range(GROUPS):
                    if before is not None:
                        pe.wait_ge(scores_read[before[0]][g], before[1] + 1)
                    mm(scores[g][:], ident_bf[:], mask[s][:].rearrange("p a b -> p (a b)"), start=True, stop=False)

            def score(s, p, n):
                c, b = divmod(n, NB)
                end = n == FC * NB - 1
                if n == 0:
                    pe.wait_ge(emptied["q_" + s], p + 1)
                    pe.wait_ge(emptied["k_" + s], p + 1)
                for g in range(GROUPS):
                    at, rows = n * P, slice(g * HD, (g + 1) * HD)
                    last = mm(scores[g][:, at:at + P], qT[s][rows, c, b, :], kT[s][rows, c, b, :],
                              start=False, stop=end)
                    if end:
                        last.then_inc(scored[s][g], 1)

            def probs_transpose(s, p, i, n):
                b, c = divmod(n, FC)
                name = f"pT{n}_{s}"
                pe.wait_ge(probs_ready[s][b], p + 1)
                take_bank(name, i)
                for g in range(GROUPS):
                    last = tr(bank(name)[:, g * P:(g + 1) * P], probs[s][:, b, c * GROUPS + g, :], ident[:])
                last.then_inc(filled[name], 1)

            def values(s, p, i, b):
                name = "o_" + s
                if b == 0:
                    take_bank(name, i)
                    pe.wait_ge(emptied["v_" + s], p + 1)
                for c in range(FC):
                    pe.wait_ge(emptied[f"pT{b * FC + c}_{s}"], p + 1)
                    for g in range(GROUPS):
                        h, at = c * GROUPS + g, (c * NB + b) * P
                        last = mm(bank(name)[g * HD:(g + 1) * HD, at:at + P], v[s][:, b, h * HD:(h + 1) * HD],
                                  pT[s][:, b, c, g * P:(g + 1) * P], start=True, stop=True)
                if b == NB - 1:
                    last.then_inc(filled[name], 1)

            def by_features(name, i, hi, lo, w_hi_, w_lo_):
                take_bank(name, i)
                for b in range(NB):
                    terms = [(x, w, c) for x, w in ((hi, w_lo_), (lo, w_hi_), (hi, w_hi_)) for c in range(FC)]
                    for n, (x, w, c) in enumerate(terms):
                        last = mm(bank(name)[:, b * D:(b + 1) * D], x[:, c, b, :], w[:, c, :],
                                  start=(n == 0), stop=(n == len(terms) - 1))
                last.then_inc(filled[name], 1)

            def output(s, p, i):
                pe.wait_ge(emptied["o_" + s], p + 1)
                by_features("proj_" + s, i, oT_hi[s], oT_lo[s], w_hi[s][:, :, 3 * D:], w_lo[s][:, :, 3 * D:])

            def iteration(i):
                if has(i, 0):
                    qkv("A", i, i)
                if has(i, 2):
                    probs_transpose("B", i - 2, i, 0)
                    probs_transpose("B", i - 2, i, 1)
                if has(i, 0):
                    score_mask("A", ("B", i - 2) if has(i, 2) else ("A", i - 1) if has(i, 1) else None)
                    score("A", i, 0)
                if has(i, 2):
                    probs_transpose("B", i - 2, i, 2)
                if has(i, 0):
                    score("A", i, 1)
                if has(i, 2):
                    probs_transpose("B", i - 2, i, 3)
                if has(i, 0):
                    score("A", i, 2)
                if has(i, 2):
                    values("B", i - 2, i, 0)
                if has(i, 0):
                    score("A", i, 3)
                if has(i, 2):
                    values("B", i - 2, i, 1)
                if has(i, 1):
                    transposed_input("B", i - 1, i)
                if has(i, 3):
                    pe.wait_ge(emptied["mix"], i - 2)
                    by_features("conv", i, mixT_hi, mixT_lo, conv_hi[:], conv_lo[:])
                if has(i, 2):
                    output("B", i - 2, i)
                if has(i, 1):
                    qkv("B", i - 1, i)
                if has(i, 0):
                    probs_transpose("A", i, i, 0)
                    probs_transpose("A", i, i, 1)
                if has(i, 2):
                    pe.wait_ge(normed["B"], i - 1)
                    take_bank("mix", i)
                    for c in range(FC):
                        for b in range(NB):
                            at = (c * NB + b) * P
                            last = mm(bank("mix")[:, at:at + P], x_in["C"][:, b, c * P:(c + 1) * P], norm_adj_T[:],
                                      start=True, stop=True)
                    last.then_inc(filled["mix"], 1)
                if has(i, 1):
                    score_mask("B", ("A", i) if has(i, 0) else ("B", i - 2))
                    score("B", i - 1, 0)
                if has(i, 0):
                    probs_transpose("A", i, i, 2)
                if has(i, 1):
                    score("B", i - 1, 1)
                if has(i, 0):
                    probs_transpose("A", i, i, 3)
                if has(i, 1):
                    score("B", i - 1, 2)
                if has(i, 0):
                    values("A", i, i, 0)
                if has(i, 1):
                    score("B", i - 1, 3)
                if has(i, 0):
                    values("A", i, i, 1)
                if has(i, -1):
                    transposed_input("A", i + 1, i)
                if has(i, 3):
                    pe.wait_ge(normed["C"], i - 2)
                    take_bank("pool", i)
                    mm(bank("pool")[:], adj_T[:], x_in["D"][:].rearrange("p b d -> p (b d)"),
                       start=True, stop=True).then_inc(filled["pool"], 1)
                if has(i, 0):
                    output("A", i, i)

            program(iteration, pe)

        @block.scalar
        def _(act):
            seen = 0
            for n, (parts, hi, _) in enumerate(weight_sets):
                seen += len(parts)
                act.wait_ge(weights_loaded, 16 * seen)
                nc.scalar.copy(hi, stage[:, :, 0:hi.shape[2]]).then_inc(weights_hi, 1)
            act.wait_ge(const_loaded, 16 * len(const_loads))

            def input_hi(s, p):
                act.wait_ge(filled["xT_" + s], p + 1)
                nc.scalar.copy(xT_hi[s][:].rearrange("p c t -> p (c t)"), bank("xT_" + s)[:]).then_inc(xT_hi_ready[s], 1)

            def save_v(s, p):
                act.wait_ge(filled["v_" + s], p + 1)
                nc.scalar.copy(v[s][:].rearrange("p b d -> p (b d)"), bank("v_" + s)[:]).then_inc(emptied["v_" + s], 1)

            def exps(s, p, b, groups):
                for g in groups:
                    if b == 0:
                        act.wait_ge(max_ready[s][g], p + 1)
                    for c in range(FC):
                        h, slot = c * GROUPS + g, c * NB + b
                        last = nc.scalar.activation(probs[s][:, b, h, :], scores[g][:, slot * P:(slot + 1) * P], ACT.Exp,
                                                    bias=neg_max[s][:, g, slot:slot + 1],
                                                    accum_out=denom[s][:, b, h:h + 1])
                    if b == NB - 1:
                        last.then_inc(scores_read[s][g], 1)
                    elif g == GROUPS - 1:
                        last.then_inc(exp_ready[s][b], 1)

            def save_probs(s, p, n):
                name = f"pT{n}_{s}"
                act.wait_ge(filled[name], p + 1)
                nc.scalar.copy(pT[s][:, n // FC, n % FC, :], bank(name)[:]).then_inc(emptied[name], 1)

            def heads_hi(s, p):
                act.wait_ge(filled["o_" + s], p + 1)
                for c in range(FC):
                    cols = slice(c * NB * P, (c + 1) * NB * P)
                    dst = oT_hi[s][:, c].rearrange("p b t -> p (b t)")
                    if s == "A":
                        last = nc.scalar.copy(dst, bank("o_A")[:, cols])
                    else:
                        last = nc.scalar.activation(dst, bank("o_B")[:, cols], ACT.Identity, bias=bv[:, c:c + 1])
                last.then_inc(oT_hi_ready[s], 1)

            def iteration(i):
                if has(i, 2):
                    exps("B", i - 2, 1, range(GROUPS))
                if has(i, 0):
                    save_v("A", i)
                if has(i, 2):
                    for n in range(NB * FC):
                        save_probs("B", i - 2, n)
                if has(i, 2):
                    heads_hi("B", i - 2)
                if has(i, 0):
                    exps("A", i, 0, range(1))
                if has(i, 1):
                    input_hi("B", i - 1)
                if has(i, 0):
                    exps("A", i, 0, range(1, GROUPS))
                    exps("A", i, 1, range(GROUPS))
                if has(i, 1):
                    save_v("B", i - 1)
                if has(i, 0):
                    save_probs("A", i, 0)
                    save_probs("A", i, 1)
                if has(i, 2):
                    act.wait_ge(filled["mix"], i - 1)
                    nc.scalar.copy(mixT_hi[:].rearrange("p c b t -> p (c b t)"), bank("mix")[:]).then_inc(mix_hi_ready, 1)
                if has(i, 0):
                    save_probs("A", i, 2)
                    save_probs("A", i, 3)
                if has(i, 0):
                    heads_hi("A", i)
                if has(i, 1):
                    exps("B", i - 1, 0, range(1))
                if has(i, -1):
                    input_hi("A", i + 1)
                if has(i, 1):
                    exps("B", i - 1, 0, range(1, GROUPS))
                if has(i, 3):
                    act.wait_ge(filled["pool"], i - 2)
                    nc.scalar.copy(pooled[:].rearrange("p b d -> p (b d)"), bank("pool")[:]).then_inc(emptied["pool"], 1)

            program(iteration, act)

        @block.vector
        def _(dve):
            tt, ts, stt = nc.vector.tensor_tensor, nc.vector.tensor_scalar, nc.vector.scalar_tensor_tensor
            dve.wait_ge(const_loaded, 16 * len(const_loads))
            adj_4 = adj[:].rearrange("p (o d) -> p o d", o=1).to_broadcast([P, GROUPS, P])
            ts(mask["A"][:], adj_4, 0.0, MASKED_A, ALU.is_equal, ALU.mult)
            ts(mask["B"][:], adj_4, 1.0, MASKED_B, ALU.subtract, ALU.mult)
            nc.vector.tensor_reduce(degree[:, 0:1], adj[:], AX_X, ALU.add).then_inc(setup_dve, 1)
            dve.wait_ge(setup_dve, 1)
            ts(degree[:, 1:2], degree[:, 0:1], 1e-30, None, ALU.max).then_inc(setup_dve, 1)
            ts(degree[:, 2:3], degree[:, 0:1], 0.0, None, ALU.is_gt).then_inc(setup_dve, 1)
            dve.wait_ge(setup_dve, 3)
            dve.wait_ge(setup_pow, 1)
            tt(degree[:, 0:1], degree[:, 3:4], degree[:, 2:3], ALU.mult).then_inc(setup_dve, 1)
            dve.wait_ge(setup_dve, 4)
            ts(row_scaled[:], adj[:], degree[:, 0:1], None, ALU.mult).then_inc(setup_dve, 1)
            dve.wait_ge(ident_ready, 1)
            nc.vector.tensor_copy(ident_bf[:], ident[:])
            dve.wait_ge(setup_pe, 1)
            nc.vector.tensor_copy(adj_T[:], scores[0][:, 0:P])
            ts(norm_adj_T[:], scores[0][:, P:2 * P], degree[:, 0:1], None, ALU.mult).then_inc(setup_done, 1)
            for n, (parts, hi, lo) in enumerate(weight_sets):
                dve.wait_ge(weights_hi, n + 1)
                tt(lo, stage[:, :, 0:lo.shape[2]], hi.bitcast(F32), ALU.subtract).then_inc(stage_split, 1)

            def input_lo(s, p):
                dve.wait_ge(xT_hi_ready[s], p + 1)
                tt(xT_lo[s][:].rearrange("p c t -> p (c t)"), bank("xT_" + s)[:],
                   xT_hi[s][:].rearrange("p c t -> p (c t)").bitcast(F32), ALU.subtract).then_inc(emptied["xT_" + s], 1)

            def row_max(s, p, groups):
                for g in groups:
                    dve.wait_ge(scored[s][g], p + 1)
                    nc.vector.tensor_reduce(neg_max[s][:, g, :], scores[g][:].rearrange("p (n k) -> p n k", k=P), AX_X,
                                            ALU.max, negate=True).then_inc(max_ready[s][g], 1)

            def save_q(s, p):
                dve.wait_ge(filled["q_" + s], p + 1)
                if s == "A":
                    ts(qT[s][:].rearrange("p c b t -> p (c b t)"), bank("q_A")[:], ATT_SCALE, None,
                       ALU.mult).then_inc(emptied["q_A"], 1)
                    return
                for c in range(FC):
                    last = ts(qT[s][:, c].rearrange("p b t -> p (b t)"), bank("q_B")[:, c * NB * P:(c + 1) * NB * P],
                              bq[:, c:c + 1], ATT_SCALE, ALU.add, ALU.mult)
                last.then_inc(emptied["q_B"], 1)

            def save_k(s, p):
                dve.wait_ge(filled["k_" + s], p + 1)
                if s == "A":
                    nc.vector.tensor_copy(kT[s][:].rearrange("p c b t -> p (c b t)"), bank("k_A")[:]).then_inc(emptied["k_A"], 1)
                    return
                for c in range(FC):
                    last = ts(kT[s][:, c].rearrange("p b t -> p (b t)"), bank("k_B")[:, c * NB * P:(c + 1) * NB * P],
                              bk[:, c:c + 1], None, ALU.add)
                last.then_inc(emptied["k_B"], 1)

            def invert(s, p, b):
                if b < NB - 1:
                    dve.wait_ge(exp_ready[s][b], p + 1)
                else:
                    dve.wait_ge(scores_read[s][GROUPS - 1], p + 1)
                nc.vector.reciprocal(inv_denom[s][:, b, :], denom[s][:, b, :]).then_inc(inv_ready[s][b], 1)

            def heads_lo(s, p):
                dve.wait_ge(oT_hi_ready[s], p + 1)
                if s == "A":
                    tt(oT_lo[s][:].rearrange("p c b t -> p (c b t)"), bank("o_A")[:],
                       oT_hi[s][:].rearrange("p c b t -> p (c b t)").bitcast(F32), ALU.subtract).then_inc(emptied["o_A"], 1)
                    return
                for c in range(FC):
                    last = stt(out=oT_lo[s][:, c].rearrange("p b t -> p (b t)"),
                               in0=bank("o_B")[:, c * NB * P:(c + 1) * NB * P], scalar=bv[:, c:c + 1],
                               in1=oT_hi[s][:, c].rearrange("p b t -> p (b t)").bitcast(F32),
                               op0=ALU.add, op1=ALU.subtract)
                last.then_inc(emptied["o_B"], 1)

            def statistics(s, p):
                dve.wait_ge(z_of[s], p + 1)
                for b in range(NB):
                    last = nc.vector.bn_stats(stats[s][:, b, :], norm_in[s][:, b, :])
                last.then_inc(stats_ready[s], 1)
                dve.wait_ge(setup_done, 1)
                dve.wait_ge(stats_ready[s], p + 1)
                for b in range(NB):
                    last = nc.vector.bn_aggr(mean_var[s][:, b, :], stats[s][:, b, :])
                last.then_inc(mean_ready[s], 1)
                dve.wait_ge(mean_ready[s], p + 1)
                ts(var_eps[s][:], mean_var[s][:, :, 1], EPS, None, ALU.add).then_inc(var_ready[s], 1)

            def normalise(s, p, taken):
                dve.wait_ge(rstd_ready[s], p + 1)
                for sem_, value in taken:
                    dve.wait_ge(sem_, value)
                for b in range(NB):
                    last = ts(norm_out[s][:, b, :], norm_in[s][:, b, :], mean_var[s][:, b, 0:1], rstd[s][:, b:b + 1],
                              ALU.subtract, ALU.mult)
                last.then_inc(normed[s], 1)

            def add_resid(s, p, name):
                dve.wait_ge(filled[name], p + 1)
                dve.wait_ge(resid_ready[s], p + 1)
                tt(z[s][:].rearrange("p b d -> p (b d)"), bank(name)[:], resid[s][:].rearrange("p b d -> p (b d)"),
                   ALU.add).then_inc(emptied[name], 1)

            def before(sem_, p, one=1):
                return [] if isinstance(p, int) and p == 0 else [(sem_, p * one)]

            def pool_layer(p):
                dve.wait_ge(emptied["pool"], p + 1)
                nc.vector.tensor_reduce(pool_max[:], pooled[:], AX_X, ALU.max)
                stt(out=pool_shift[:].rearrange("p b d -> p (b d)"), in0=pooled[:].rearrange("p b d -> p (b d)"),
                    scalar=b_pool[:, 0:1], in1=pooled[:].rearrange("p b d -> p (b d)"),
                    op0=ALU.add, op1=ALU.subtract).then_inc(pool_shift_ready, 1)
                dve.wait_ge(pool_shift_ready, p + 1)
                for b in range(NB):
                    last = ts(pool_relu[:, b, :], pool_shift[:, b, :], pool_max[:, b:b + 1], 0.0, ALU.add, ALU.max)
                last.then_inc(pool_relu_ready, 1)
                dve.wait_ge(pool_relu_ready, p + 1)
                tt(z["D"][:], pool_relu[:], x_in["D"][:], ALU.add).then_inc(z_ready["D"], 1)

            def iteration(i):
                if has(i, 1):
                    dve.wait_ge(filled["proj_A"], i)
                    tt(att_out[:], bank("proj_A")[:].rearrange("p (b d) -> p b d", b=NB), everywhere(b_proj),
                       ALU.add).then_inc(emptied["proj_A"], 1)
                if has(i, 1):
                    statistics("I", i - 1)
                if has(i, 0):
                    save_q("A", i)
                if has(i, 2):
                    invert("B", i - 2, 1)
                if has(i, 1):
                    for b in range(NB):
                        last = stt(out=centred[:, b, :], in0=att_out[:, b, :], scalar=mean_var["I"][:, b, 0:1],
                                   in1=gamma[:], op0=ALU.subtract, op1=ALU.mult)
                    last.then_inc(centred_ready, 1)
                if has(i, 0):
                    save_k("A", i)
                if has(i, 4):
                    pool_layer(i - 4)
                if has(i, 1):
                    dve.wait_ge(centred_ready, i)
                    dve.wait_ge(rstd_ready["I"], i)
                    dve.wait_ge(pre_sum_ready, i)
                    for b in range(NB):
                        last = stt(out=z["A"][:, b, :], in0=centred[:, b, :], scalar=rstd["I"][:, b:b + 1],
                                   in1=pre_sum[:, b, :], op0=ALU.mult, op1=ALU.add)
                    last.then_inc(z_ready["A"], 1)
                    statistics("A", i - 1)
                if has(i, 4):
                    statistics("D", i - 4)
                if has(i, 1):
                    normalise("A", i - 1, before(filled["xT_B"], i - 1) + before(resid_ready["B"], i - 1))
                if has(i, 0):
                    row_max("A", i, range(2))
                if has(i, 2):
                    heads_lo("B", i - 2)
                if has(i, 0):
                    row_max("A", i, range(2, GROUPS))
                if has(i, 1):
                    input_lo("B", i - 1)
                if has(i, 4):
                    normalise("D", i - 4, before(result_stored, i - 4, 16))
                if has(i, 0):
                    invert("A", i, 0)
                if has(i, 3):
                    add_resid("C", i - 3, "conv")
                if has(i, 2):
                    add_resid("B", i - 2, "proj_B")
                    statistics("B", i - 2)
                if has(i, 1):
                    save_q("B", i - 1)
                if has(i, 0):
                    invert("A", i, 1)
                if has(i, 2):
                    normalise("B", i - 2, before(filled["mix"], i - 2) + before(resid_ready["C"], i - 2))
                if has(i, 1):
                    save_k("B", i - 1)
                if has(i, 3):
                    statistics("C", i - 3)
                if has(i, 2):
                    dve.wait_ge(mix_hi_ready, i - 1)
                    tt(mixT_lo[:].rearrange("p c b t -> p (c b t)"), bank("mix")[:],
                       mixT_hi[:].rearrange("p c b t -> p (c b t)").bitcast(F32), ALU.subtract).then_inc(emptied["mix"], 1)
                if has(i, 3):
                    normalise("C", i - 3, before(filled["pool"], i - 3) + before(z_ready["D"], i - 3))
                if has(i, 1):
                    row_max("B", i - 1, range(2))
                if has(i, 0):
                    heads_lo("A", i)
                if has(i, 1):
                    row_max("B", i - 1, range(2, GROUPS))
                if has(i, -1):
                    input_lo("A", i + 1)
                if has(i, 1):
                    invert("B", i - 1, 0)

            program(iteration, dve)

        @block.gpsimd
        def _(pool):
            tt = nc.gpsimd.tensor_tensor
            nc.gpsimd.memset(minus_half[:], -0.5)
            nc.gpsimd.memset(ident[:], 0.0).then_inc(ident_zero, 1)
            pool.wait_ge(ident_zero, 1)
            nc.gpsimd.affine_select(out=ident[:], in_=ident[:], compare_op=ALU.not_equal, fill=1.0, base=0,
                                    pattern=[[-1, P]], channel_multiplier=1).then_inc(ident_ready, 1)
            pool.wait_ge(const_loaded, 16 * len(const_loads))
            pool.wait_ge(ident_ready, 1)
            pool.wait_ge(setup_dve, 3)
            tt(degree[:, 3:4], degree[:, 1:2], minus_half[:, 0:1], ALU.pow).then_inc(setup_pow, 1)

            def residual(s, p, ready, value, bias):
                pool.wait_ge(ready, value)
                if s != "A" and not (isinstance(p, int) and p == 0):
                    pool.wait_ge(emptied["proj_B" if s == "B" else "conv"], p)
                if s == "A" and not (isinstance(p, int) and p == 0):
                    pool.wait_ge(pre_sum_ready, p)
                tt(resid[s][:], x_in[s][:], everywhere(bias), ALU.add).then_inc(resid_ready[s], 1)

            def scale_probs(s, p, b):
                pool.wait_ge(inv_ready[s][b], p + 1)
                tt(probs[s][:, b], probs[s][:, b],
                   inv_denom[s][:, b, :].rearrange("p (h o) -> p h o", o=1).to_broadcast([P, HEADS, P]),
                   ALU.mult).then_inc(probs_ready[s][b], 1)

            def inverse_root(s, p):
                pool.wait_ge(var_ready[s], p + 1)
                tt(rstd[s][:], var_eps[s][:], minus_half[:], ALU.pow).then_inc(rstd_ready[s], 1)

            def iteration(i):
                if has(i, 1):
                    inverse_root("I", i - 1)
                if has(i, 2):
                    scale_probs("B", i - 2, 1)
                if has(i, 1):
                    pool.wait_ge(emptied["proj_A"], i)
                    pool.wait_ge(resid_ready["A"], i)
                    if not (isinstance(i, int) and i == 1):
                        pool.wait_ge(z_ready["A"], i - 1)
                    tt(pre_sum[:], att_out[:], resid["A"][:], ALU.add).then_inc(pre_sum_ready, 1)
                if has(i, 1):
                    inverse_root("A", i - 1)
                if has(i, 0):
                    residual("A", i, x_loaded, 16 * (i + 1), beta)
                if has(i, 4):
                    inverse_root("D", i - 4)
                if has(i, 0):
                    scale_probs("A", i, 0)
                if has(i, 2):
                    inverse_root("B", i - 2)
                if has(i, 1):
                    residual("B", i - 1, normed["A"], i, b_out)
                if has(i, 0):
                    scale_probs("A", i, 1)
                if has(i, 3):
                    inverse_root("C", i - 3)
                if has(i, 2):
                    residual("C", i - 2, normed["B"], i - 1, b_conv)
                if has(i, 1):
                    scale_probs("B", i - 1, 0)

            program(iteration, pool)


_NAMES = ["x", "adj", "L0_gnn_w_qkv", "L0_gnn_w_proj", "L0_gnn_b_proj", "L0_gnn_ln_gamma", "L0_gnn_ln_beta",
          "L1_gnn_Wq", "L1_gnn_bq", "L1_gnn_Wk", "L1_gnn_bk", "L1_gnn_Wv", "L1_gnn_bv", "L1_gnn_Wo", "L1_gnn_bo",
          "L2_gnn_weight", "L2_gnn_bias", "L3_gnn_b"]


def kernel(**inputs):
    import numpy as np
    import concourse.bacc as bacc
    from concourse.bass_utils import run_bass_kernel_spmd

    nc = bacc.Bacc("TRN2", target_bir_lowering=False, num_devices=1)
    arrays, args = {}, {}
    for name in _NAMES:
        arr = np.ascontiguousarray(inputs[name])
        arrays[f"in_{name}"] = arr
        args[name] = nc.dram_tensor(f"in_{name}", arr.shape, mybir.dt.from_np(arr.dtype), kind="ExternalInput").ap()
    shape = arrays["in_x"].shape
    out = nc.dram_tensor("out", shape, F32, kind="ExternalOutput").ap()
    gnn_kernel(nc, args, out, shape[0])
    return run_bass_kernel_spmd(nc, [arrays], core_ids=[0]).results[0]["out"]
```

```python
from contextlib import ExitStack

import concourse.bass as bass
from concourse import mybir

F32 = mybir.dt.float32
F32R = mybir.dt.float32r
BF16 = mybir.dt.bfloat16
ALU = mybir.AluOpType
ACT = mybir.ActivationFunctionType
AX_X = mybir.AxisListType.X

P = 128
D = 256
FC = D // P
HEADS = 8
HD = D // HEADS
GROUPS = P // HD
NB = 2
EPS = 1e-5
ATT_SCALE = float(HD) ** -0.5
MASKED_A = -1e38
MASKED_B = 1e9

RING = [
    ("q_A", 0), ("k_A", 0), ("v_A", 0),
    ("pT0_B", 2), ("pT1_B", 2), ("pT2_B", 2), ("pT3_B", 2), ("o_B", 2),
    ("xT_B", 1), ("conv", 3), ("proj_B", 2),
    ("q_B", 1), ("k_B", 1), ("v_B", 1),
    ("pT0_A", 0), ("pT1_A", 0), ("pT2_A", 0), ("pT3_A", 0), ("mix", 2), ("o_A", 0),
    ("pool", 3), ("xT_A", -1), ("proj_A", 0),
]
RING_AT = {name: n for n, (name, _) in enumerate(RING)}
RING_BANKS = 4
LAST_LAG = 4
FIRST_LOOPED = LAST_LAG + 1


def gnn_kernel(nc, a, out, batches):
    pairs = batches // NB

    def has(i, lag):
        return not isinstance(i, int) or 0 <= i - lag < pairs

    def last_holder(name, i):
        at = RING_AT[name]
        back = 0
        while back < 8:
            at -= 1
            if at < 0:
                at += len(RING)
                back += 1
            if at % RING_BANKS == RING_AT[name] % RING_BANKS and has(i - back if back else i, RING[at][1]):
                if isinstance(i, int) and i - back < -1:
                    return None
                return RING[at][0], i - back - RING[at][1]
        return None

    with ExitStack() as ctx:
        def sb(name, shape, dt=F32):
            return ctx.enter_context(nc.sbuf_tensor(name, shape, dt))

        def sem(name):
            return ctx.enter_context(nc.semaphore(name))

        ident = sb("ident", [P, P])
        ident_bf = sb("ident_bf", [P, P], BF16)
        adj = sb("adj", [P, P])
        adj_T = sb("adj_T", [P, P])
        norm_adj_T = sb("norm_adj_T", [P, P])
        row_scaled = sb("row_scaled", [P, P])
        degree = sb("degree", [P, 4])
        mask = {s: sb(f"mask_{s}", [P, GROUPS, P], BF16) for s in "AB"}
        minus_half = sb("minus_half", [P, NB])
        stage = {s: sb(f"stage_{s}", [P, FC, width]) for s, width in (("A", 4 * D), ("B", 4 * D), ("conv", D))}
        w_hi = {s: sb(f"w_hi_{s}", [P, FC, 4 * D], F32R) for s in "AB"}
        w_lo = {s: sb(f"w_lo_{s}", [P, FC, 4 * D], F32R) for s in "AB"}
        conv_hi = sb("conv_hi", [P, FC, D], F32R)
        conv_lo = sb("conv_lo", [P, FC, D], F32R)
        b_proj = sb("b_proj", [P, D])
        gamma = sb("gamma", [P, D])
        beta = sb("beta", [P, D])
        b_last = sb("b_last", [P, D])
        b_out = sb("b_out", [P, D])
        b_conv = sb("b_conv", [P, D])
        bq = sb("bq", [P, FC])
        bk = sb("bk", [P, FC])
        bv = sb("bv", [P, FC])
        b_pool = sb("b_pool", [P, 1])

        x_in = {s: sb(f"x_in_{s}", [P, NB, D]) for s in "ABCD"}
        resid = {s: sb(f"resid_{s}", [P, NB, D]) for s in "ABC"}
        xT_hi = {s: sb(f"xT_hi_{s}", [P, FC, NB * P], F32R) for s in "AB"}
        xT_lo = {s: sb(f"xT_lo_{s}", [P, FC, NB * P], F32R) for s in "AB"}
        qT = {s: sb(f"qT_{s}", [P, FC, NB, P]) for s in "AB"}
        kT = {s: sb(f"kT_{s}", [P, FC, NB, P]) for s in "AB"}
        v = {s: sb(f"v_{s}", [P, NB, D]) for s in "AB"}
        neg_max = {s: sb(f"neg_max_{s}", [P, GROUPS, FC * NB]) for s in "AB"}
        probs = {s: sb(f"probs_{s}", [P, NB, HEADS, P]) for s in "AB"}
        denom = {s: sb(f"denom_{s}", [P, NB, HEADS]) for s in "AB"}
        inv_denom = {s: sb(f"inv_denom_{s}", [P, NB, HEADS]) for s in "AB"}
        pT = {s: sb(f"pT_{s}", [P, NB, FC, GROUPS * P]) for s in "AB"}
        oT_hi = {s: sb(f"oT_hi_{s}", [P, FC, NB, P], F32R) for s in "AB"}
        oT_lo = {s: sb(f"oT_lo_{s}", [P, FC, NB, P], F32R) for s in "AB"}
        mixT_hi = sb("mixT_hi", [P, FC, NB, P], F32R)
        mixT_lo = sb("mixT_lo", [P, FC, NB, P], F32R)
        att_out = sb("att_out", [P, NB, D])
        centred = sb("centred", [P, NB, D])
        pre_sum = sb("pre_sum", [P, NB, D])
        z = {s: sb(f"z_{s}", [P, NB, D]) for s in "ABCD"}
        pooled = sb("pooled", [P, NB, D])
        pool_shift = sb("pool_shift", [P, NB, D])
        pool_relu = sb("pool_relu", [P, NB, D])
        pool_max = sb("pool_max", [P, NB])
        norm_of = "IABCD"
        stats = {s: sb(f"stats_{s}", [P, NB, 6]) for s in norm_of}
        mean_var = {s: sb(f"mean_var_{s}", [P, NB, 2]) for s in norm_of}
        var_eps = {s: sb(f"var_eps_{s}", [P, NB]) for s in norm_of}
        rstd = {s: sb(f"rstd_{s}", [P, NB]) for s in norm_of}
        result = sb("result", [P, NB, D])

        scores = [ctx.enter_context(nc.psum_tensor(f"scores{g}", [P, 512], F32)) for g in range(GROUPS)]
        ring = [ctx.enter_context(nc.psum_tensor(f"ring{n}", [P, 512], F32)) for n in range(RING_BANKS)]

        def bank(name):
            return ring[RING_AT[name] % RING_BANKS]

        adj_loaded = sem("adj_loaded")
        const_loaded = sem("const_loaded")
        weights_loaded = {name: sem(f"weights_loaded_{name}") for name in ("qkv_A", "out_A", "B", "conv")}
        stage_split = sem("stage_split")
        ident_zero = sem("ident_zero")
        ident_ready = sem("ident_ready")
        setup_dve = sem("setup_dve")
        setup_pow = sem("setup_pow")
        setup_bias = sem("setup_bias")
        setup_pe = sem("setup_pe")
        setup_done = sem("setup_done")
        weights_hi = sem("weights_hi")
        x_loaded = sem("x_loaded")
        result_stored = sem("result_stored")
        filled = {name: sem(f"filled_{name}") for name, _ in RING}
        emptied = {name: sem(f"emptied_{name}") for name, _ in RING}
        xT_hi_ready = {s: sem(f"xT_hi_ready_{s}") for s in "AB"}
        oT_hi_ready = {s: sem(f"oT_hi_ready_{s}") for s in "AB"}
        mix_hi_ready = sem("mix_hi_ready")
        scored = {s: [sem(f"scored_{s}{g}") for g in range(GROUPS)] for s in "AB"}
        max_ready = {s: [sem(f"max_ready_{s}{g}") for g in range(GROUPS)] for s in "AB"}
        scores_read = {s: [sem(f"scores_read_{s}{g}") for g in range(GROUPS)] for s in "AB"}
        exp_ready = {s: [sem(f"exp_ready_{s}{b}") for b in range(NB)] for s in "AB"}
        inv_ready = {s: [sem(f"inv_ready_{s}{b}") for b in range(NB)] for s in "AB"}
        probs_ready = {s: [sem(f"probs_ready_{s}{n}") for n in range(NB * FC)] for s in "AB"}
        resid_ready = {s: sem(f"resid_ready_{s}") for s in "ABC"}
        att_out_ready = sem("att_out_ready")
        centred_ready = sem("centred_ready")
        z_ready = {s: sem(f"z_ready_{s}") for s in "AD"}
        stats_ready = {s: sem(f"stats_ready_{s}") for s in norm_of}
        mean_ready = {s: sem(f"mean_ready_{s}") for s in norm_of}
        var_ready = {s: sem(f"var_ready_{s}") for s in norm_of}
        rstd_ready = {s: sem(f"rstd_ready_{s}") for s in norm_of}
        normed = {s: sem(f"normed_{s}") for s in "ABCD"}
        pool_shift_ready = sem("pool_shift_ready")
        pool_relu_ready = sem("pool_relu_ready")
        z_of = {"I": att_out_ready, "A": z_ready["A"], "B": emptied["proj_B"], "C": emptied["conv"],
                "D": z_ready["D"]}
        norm_in = {"I": att_out, **z}
        norm_out = {"A": x_in["B"], "B": x_in["C"], "C": x_in["D"], "D": result}

        def row(name):
            return a[name].rearrange("(o d) -> o d", o=1).to_broadcast([P, D])

        def column(name, c):
            return a[name][c * P:(c + 1) * P].rearrange("(p o) -> p o", o=1)

        def chunked(name):
            return a[name].rearrange("(c p) n -> p c n", p=P)

        def everywhere(t):
            return t[:].rearrange("p (o d) -> p o d", o=1).to_broadcast([P, NB, D])

        x_dram = a["x"].rearrange("(n b) t d -> n t b d", b=NB)
        out_dram = out.rearrange("(n b) t d -> n t b d", b=NB)

        const_loads = [
            (b_proj[:], row("L0_gnn_b_proj")), (gamma[:], row("L0_gnn_ln_gamma")),
            (beta[:], row("L0_gnn_ln_beta")), (b_out[:], row("L1_gnn_bo")), (b_conv[:], row("L2_gnn_bias")),
            (b_pool[:], column("L3_gnn_b", 0)),
        ] + [(dst[:, c:c + 1], column(name, c)) for dst, name in ((bq, "L1_gnn_bq"), (bk, "L1_gnn_bk"), (bv, "L1_gnn_bv"))
             for c in range(FC)]
        w_qkv = chunked("L0_gnn_w_qkv")

        def blk(n):
            return slice(n * D, (n + 1) * D)

        weight_blocks = [
            (w_qkv[:, :, blk(n)], stage["A"][:, :, blk(n)], w_hi["A"][:, :, blk(n)], w_lo["A"][:, :, blk(n)], "qkv_A", 3)
            for n in range(3)
        ] + [
            (chunked("L0_gnn_w_proj"), stage["A"][:, :, blk(3)], w_hi["A"][:, :, blk(3)], w_lo["A"][:, :, blk(3)],
             "out_A", 1)
        ] + [
            (chunked(name), stage["B"][:, :, blk(n)], w_hi["B"][:, :, blk(n)], w_lo["B"][:, :, blk(n)], "B", 4)
            for n, name in enumerate(("L1_gnn_Wq", "L1_gnn_Wk", "L1_gnn_Wv", "L1_gnn_Wo"))
        ] + [(chunked("L2_gnn_weight"), stage["conv"][:], conv_hi[:], conv_lo[:], "conv", 1)]
        BLOCKS_A, BLOCKS_B = 4, 8

        def program(iteration, eng, late_setup=None):
            iteration(-1)
            if late_setup:
                late_setup()
            for i in range(FIRST_LOOPED):
                iteration(i)
            with eng.Fori(FIRST_LOOPED, pairs - 1) as i:
                iteration(i)
            for i in range(pairs - 1, pairs + LAST_LAG):
                iteration(i)

        block = ctx.enter_context(nc.Block())

        @block.sync
        def _(sp):
            sp.dma_start(adj[:], a["adj"]).then_inc(adj_loaded, 16)
            sp.dma_start(x_in["A"][:], x_dram[0]).then_inc(x_loaded, 16)
            for src, dst, _, _, name, _ in weight_blocks[:BLOCKS_A]:
                sp.dma_start(dst, src).then_inc(weights_loaded[name], 16)
            for dst, src in const_loads:
                sp.dma_start(dst, src).then_inc(const_loaded, 16)
            for src, dst, _, _, name, _ in weight_blocks[BLOCKS_A:]:
                sp.dma_start(dst, src).then_inc(weights_loaded[name], 16)

            def iteration(i):
                if has(i, -1) and not (isinstance(i, int) and i == -1):
                    sp.wait_ge(filled["xT_A"], i + 1)
                    sp.wait_ge(resid_ready["A"], i + 1)
                    sp.dma_start(x_in["A"][:], x_dram[i + 1]).then_inc(x_loaded, 16)
                if has(i, 4):
                    sp.wait_ge(normed["D"], i - 3)
                    sp.dma_start(out_dram[i - 4], result[:]).then_inc(result_stored, 16)

            program(iteration, sp)
            sp.wait_ge(result_stored, 16 * pairs)

        @block.tensor
        def _(pe):
            mm, tr = nc.tensor.matmul, nc.tensor.transpose
            pe.wait_ge(ident_ready, 1)

            def late_setup():
                pe.wait_ge(adj_loaded, 16)
                tr(scores[0][:, 0:P], adj[:], ident[:])
                pe.wait_ge(setup_dve, 5)
                tr(scores[0][:, P:2 * P], row_scaled[:], ident[:]).then_inc(setup_pe, 1)

            def first_use(p, blocks):
                if isinstance(p, int) and p == 0:
                    pe.wait_ge(stage_split, blocks)

            def take_bank(name, i):
                held = last_holder(name, i)
                if held:
                    pe.wait_ge(emptied[held[0]], held[1] + 1)

            def transposed_input(s, p, i):
                name = "xT_" + s
                if s == "A":
                    pe.wait_ge(x_loaded, 16 * (p + 1))
                else:
                    pe.wait_ge(normed["A"], p + 1)
                take_bank(name, i)
                for c in range(FC):
                    for b in range(NB):
                        at = (c * NB + b) * P
                        last = tr(bank(name)[:, at:at + P], x_in[s][:, b, c * P:(c + 1) * P], ident[:])
                last.then_inc(filled[name], 1)

            def qkv(s, p, i):
                pe.wait_ge(xT_hi_ready[s], p + 1)
                for part, name in enumerate(("q_" + s, "k_" + s)):
                    first_use(p, (0 if s == "A" else BLOCKS_A) + part + 1)
                    take_bank(name, i)
                    for oc in range(FC):
                        cols = slice(part * D + oc * P, part * D + (oc + 1) * P)
                        terms = [(w, x, c) for w, x in ((w_lo[s], xT_hi[s]), (w_hi[s], xT_hi[s]), (w_hi[s], xT_lo[s]))
                                 for c in range(FC)]
                        for n, (w, x, c) in enumerate(terms):
                            if part == 0 and oc == 0 and n == 2 * FC:
                                pe.wait_ge(emptied["xT_" + s], p + 1)
                            last = mm(bank(name)[:, oc * NB * P:(oc + 1) * NB * P], w[:, c, cols], x[:, c, :],
                                      start=(n == 0), stop=(n == len(terms) - 1))
                    last.then_inc(filled[name], 1)
                name = "v_" + s
                first_use(p, (0 if s == "A" else BLOCKS_A) + 3)
                take_bank(name, i)
                for b in range(NB):
                    terms = [(x, w, c) for x, w in ((xT_hi[s], w_lo[s]), (xT_hi[s], w_hi[s]), (xT_lo[s], w_hi[s]))
                             for c in range(FC)]
                    for n, (x, w, c) in enumerate(terms):
                        last = mm(bank(name)[:, b * D:(b + 1) * D], x[:, c, b * P:(b + 1) * P],
                                  w[:, c, 2 * D:3 * D], start=(n == 0), stop=(n == len(terms) - 1))
                last.then_inc(filled[name], 1)

            def score_mask(s, before):
                if before is None:
                    pe.wait_ge(setup_done, 1)
                for g in range(GROUPS):
                    if before is not None:
                        pe.wait_ge(scores_read[before[0]][g], before[1] + 1)
                    mm(scores[g][:], ident_bf[:], mask[s][:].rearrange("p a b -> p (a b)"), start=True, stop=False)

            def score(s, p, n):
                c, b = divmod(n, NB)
                end = n == FC * NB - 1
                if n == 0:
                    pe.wait_ge(emptied["q_" + s], p + 1)
                    pe.wait_ge(emptied["k_" + s], p + 1)
                for g in range(GROUPS):
                    at, rows = n * P, slice(g * HD, (g + 1) * HD)
                    last = mm(scores[g][:, at:at + P], qT[s][rows, c, b, :], kT[s][rows, c, b, :],
                              start=False, stop=end)
                    if end:
                        last.then_inc(scored[s][g], 1)

            def probs_transpose(s, p, i, n):
                b, c = divmod(n, FC)
                name = f"pT{n}_{s}"
                pe.wait_ge(probs_ready[s][n], p + 1)
                take_bank(name, i)
                for g in range(GROUPS):
                    last = tr(bank(name)[:, g * P:(g + 1) * P], probs[s][:, b, c * GROUPS + g, :], ident[:])
                last.then_inc(filled[name], 1)

            def values(s, p, i, b):
                name = "o_" + s
                if b == 0:
                    take_bank(name, i)
                    pe.wait_ge(emptied["v_" + s], p + 1)
                for c in range(FC):
                    pe.wait_ge(emptied[f"pT{b * FC + c}_{s}"], p + 1)
                    for g in range(GROUPS):
                        h, at = c * GROUPS + g, (c * NB + b) * P
                        last = mm(bank(name)[g * HD:(g + 1) * HD, at:at + P], v[s][:, b, h * HD:(h + 1) * HD],
                                  pT[s][:, b, c, g * P:(g + 1) * P], start=True, stop=True)
                if b == NB - 1:
                    last.then_inc(filled[name], 1)

            def by_features(name, i, hi, lo, w_hi_, w_lo_, lo_ready, value):
                take_bank(name, i)
                for b in range(NB):
                    terms = [(x, w, c) for x, w in ((hi, w_lo_), (hi, w_hi_), (lo, w_hi_)) for c in range(FC)]
                    for n, (x, w, c) in enumerate(terms):
                        if b == 0 and n == 2 * FC:
                            pe.wait_ge(lo_ready, value)
                        last = mm(bank(name)[:, b * D:(b + 1) * D], x[:, c, b, :], w[:, c, :],
                                  start=(n == 0), stop=(n == len(terms) - 1))
                last.then_inc(filled[name], 1)

            def output(s, p, i):
                first_use(p, BLOCKS_A if s == "A" else BLOCKS_B)
                pe.wait_ge(oT_hi_ready[s], p + 1)
                by_features("proj_" + s, i, oT_hi[s], oT_lo[s], w_hi[s][:, :, 3 * D:], w_lo[s][:, :, 3 * D:],
                            emptied["o_" + s], p + 1)

            def iteration(i):
                if has(i, 0):
                    qkv("A", i, i)
                if has(i, 2):
                    probs_transpose("B", i - 2, i, 0)
                    probs_transpose("B", i - 2, i, 1)
                if has(i, 0):
                    score_mask("A", ("B", i - 2) if has(i, 2) else ("A", i - 1) if has(i, 1) else None)
                    score("A", i, 0)
                if has(i, 2):
                    probs_transpose("B", i - 2, i, 2)
                if has(i, 0):
                    score("A", i, 1)
                if has(i, 2):
                    probs_transpose("B", i - 2, i, 3)
                if has(i, 0):
                    score("A", i, 2)
                if has(i, 0):
                    score("A", i, 3)
                if has(i, 2):
                    values("B", i - 2, i, 0)
                    values("B", i - 2, i, 1)
                if has(i, 1):
                    transposed_input("B", i - 1, i)
                if has(i, 3):
                    first_use(i - 3, len(weight_blocks))
                    pe.wait_ge(mix_hi_ready, i - 2)
                    by_features("conv", i, mixT_hi, mixT_lo, conv_hi[:], conv_lo[:], emptied["mix"], i - 2)
                if has(i, 2):
                    output("B", i - 2, i)
                if has(i, 1):
                    qkv("B", i - 1, i)
                if has(i, 0):
                    probs_transpose("A", i, i, 0)
                    probs_transpose("A", i, i, 1)
                if has(i, 1):
                    score_mask("B", ("A", i) if has(i, 0) else ("B", i - 2))
                    score("B", i - 1, 0)
                if has(i, 0):
                    probs_transpose("A", i, i, 2)
                if has(i, 1):
                    score("B", i - 1, 1)
                if has(i, 0):
                    probs_transpose("A", i, i, 3)
                if has(i, 1):
                    score("B", i - 1, 2)
                if has(i, 2):
                    pe.wait_ge(normed["B"], i - 1)
                    take_bank("mix", i)
                    for c in range(FC):
                        for b in range(NB):
                            at = (c * NB + b) * P
                            last = mm(bank("mix")[:, at:at + P], x_in["C"][:, b, c * P:(c + 1) * P], norm_adj_T[:],
                                      start=True, stop=True)
                    last.then_inc(filled["mix"], 1)
                if has(i, 1):
                    score("B", i - 1, 3)
                if has(i, 0):
                    values("A", i, i, 0)
                    values("A", i, i, 1)
                if has(i, 3):
                    pe.wait_ge(normed["C"], i - 2)
                    take_bank("pool", i)
                    mm(bank("pool")[:], adj_T[:], x_in["D"][:].rearrange("p b d -> p (b d)"),
                       start=True, stop=True).then_inc(filled["pool"], 1)
                if has(i, -1):
                    transposed_input("A", i + 1, i)
                if has(i, 0):
                    output("A", i, i)

            program(iteration, pe, late_setup)

        @block.scalar
        def _(act):
            def split_weights(blocks):
                for _, staged, hi, _, name, loads in blocks:
                    act.wait_ge(weights_loaded[name], 16 * loads)
                    nc.scalar.copy(hi, staged).then_inc(weights_hi, 1)

            def late_setup():
                split_weights(weight_blocks[BLOCKS_A:])
                act.wait_ge(const_loaded, 16 * len(const_loads))

            split_weights(weight_blocks[:BLOCKS_A])

            def input_hi(s, p):
                act.wait_ge(filled["xT_" + s], p + 1)
                nc.scalar.copy(xT_hi[s][:].rearrange("p c t -> p (c t)"), bank("xT_" + s)[:]).then_inc(xT_hi_ready[s], 1)

            def save_q_a(p):
                act.wait_ge(filled["q_A"], p + 1)
                nc.scalar.mul(qT["A"][:].rearrange("p c b t -> p (c b t)"), bank("q_A")[:],
                              ATT_SCALE).then_inc(emptied["q_A"], 1)

            def save_k_a(p):
                act.wait_ge(filled["k_A"], p + 1)
                nc.scalar.copy(kT["A"][:].rearrange("p c b t -> p (c b t)"), bank("k_A")[:]).then_inc(emptied["k_A"], 1)

            def save_k_b(p):
                act.wait_ge(filled["k_B"], p + 1)
                for c in range(FC):
                    last = nc.scalar.activation(kT["B"][:, c].rearrange("p b t -> p (b t)"),
                                                bank("k_B")[:, c * NB * P:(c + 1) * NB * P], ACT.Identity,
                                                bias=bk[:, c:c + 1])
                last.then_inc(emptied["k_B"], 1)

            def save_v(s, p):
                act.wait_ge(filled["v_" + s], p + 1)
                nc.scalar.copy(v[s][:].rearrange("p b d -> p (b d)"), bank("v_" + s)[:]).then_inc(emptied["v_" + s], 1)

            def exps(s, p, b, groups):
                for g in groups:
                    if b == 0:
                        act.wait_ge(max_ready[s][g], p + 1)
                    for c in range(FC):
                        h, slot = c * GROUPS + g, c * NB + b
                        last = nc.scalar.activation(probs[s][:, b, h, :], scores[g][:, slot * P:(slot + 1) * P], ACT.Exp,
                                                    bias=neg_max[s][:, g, slot:slot + 1],
                                                    accum_out=denom[s][:, b, h:h + 1])
                    if b == NB - 1:
                        last.then_inc(scores_read[s][g], 1)
                    elif g == GROUPS - 1:
                        last.then_inc(exp_ready[s][b], 1)

            def save_probs(s, p, n):
                name = f"pT{n}_{s}"
                act.wait_ge(filled[name], p + 1)
                nc.scalar.copy(pT[s][:, n // FC, n % FC, :], bank(name)[:]).then_inc(emptied[name], 1)

            def heads_hi(s, p):
                act.wait_ge(filled["o_" + s], p + 1)
                for c in range(FC):
                    cols = slice(c * NB * P, (c + 1) * NB * P)
                    dst = oT_hi[s][:, c].rearrange("p b t -> p (b t)")
                    if s == "A":
                        last = nc.scalar.copy(dst, bank("o_A")[:, cols])
                    else:
                        last = nc.scalar.activation(dst, bank("o_B")[:, cols], ACT.Identity, bias=bv[:, c:c + 1])
                last.then_inc(oT_hi_ready[s], 1)

            def iteration(i):
                if has(i, 2):
                    exps("B", i - 2, 1, range(2))
                if has(i, 0):
                    save_q_a(i)
                if has(i, 2):
                    exps("B", i - 2, 1, range(2, GROUPS))
                if has(i, 0):
                    save_k_a(i)
                    save_v("A", i)
                if has(i, 2):
                    for n in range(NB * FC):
                        save_probs("B", i - 2, n)
                    heads_hi("B", i - 2)
                if has(i, 0):
                    exps("A", i, 0, range(1))
                if has(i, 1):
                    input_hi("B", i - 1)
                if has(i, 0):
                    exps("A", i, 0, range(1, GROUPS))
                    exps("A", i, 1, range(GROUPS))
                if has(i, 1):
                    save_k_b(i - 1)
                    save_v("B", i - 1)
                if has(i, 0):
                    for n in range(NB * FC):
                        save_probs("A", i, n)
                if has(i, 2):
                    act.wait_ge(filled["mix"], i - 1)
                    nc.scalar.copy(mixT_hi[:].rearrange("p c b t -> p (c b t)"), bank("mix")[:]).then_inc(mix_hi_ready, 1)
                if has(i, 0):
                    heads_hi("A", i)
                if has(i, 1):
                    exps("B", i - 1, 0, range(1))
                if has(i, -1):
                    input_hi("A", i + 1)
                if has(i, 3):
                    act.wait_ge(filled["pool"], i - 2)
                    nc.scalar.copy(pooled[:].rearrange("p b d -> p (b d)"), bank("pool")[:]).then_inc(emptied["pool"], 1)
                if has(i, 1):
                    exps("B", i - 1, 0, range(1, GROUPS))

            program(iteration, act, late_setup)

        @block.vector
        def _(dve):
            tt, ts, stt = nc.vector.tensor_tensor, nc.vector.tensor_scalar, nc.vector.scalar_tensor_tensor
            dve.wait_ge(adj_loaded, 16)
            adj_4 = adj[:].rearrange("p (o d) -> p o d", o=1).to_broadcast([P, GROUPS, P])
            ts(mask["A"][:], adj_4, 0.0, MASKED_A, ALU.is_equal, ALU.mult)
            ts(mask["B"][:], adj_4, 1.0, MASKED_B, ALU.subtract, ALU.mult)
            nc.vector.tensor_reduce(degree[:, 0:1], adj[:], AX_X, ALU.add).then_inc(setup_dve, 1)
            dve.wait_ge(setup_dve, 1)
            ts(degree[:, 1:2], degree[:, 0:1], 1e-30, None, ALU.max).then_inc(setup_dve, 1)
            ts(degree[:, 2:3], degree[:, 0:1], 0.0, None, ALU.is_gt).then_inc(setup_dve, 1)
            dve.wait_ge(setup_dve, 3)
            dve.wait_ge(setup_pow, 1)
            tt(degree[:, 0:1], degree[:, 3:4], degree[:, 2:3], ALU.mult).then_inc(setup_dve, 1)
            dve.wait_ge(setup_dve, 4)
            ts(row_scaled[:], adj[:], degree[:, 0:1], None, ALU.mult).then_inc(setup_dve, 1)
            dve.wait_ge(ident_ready, 1)
            nc.vector.tensor_copy(ident_bf[:], ident[:])

            def split_weights(first, end):
                for n in range(first, end):
                    _, staged, hi, lo, _, _ = weight_blocks[n]
                    dve.wait_ge(weights_hi, n + 1)
                    tt(lo, staged, hi.bitcast(F32), ALU.subtract).then_inc(stage_split, 1)

            def late_setup():
                dve.wait_ge(setup_pe, 1)
                nc.vector.tensor_copy(adj_T[:], scores[0][:, 0:P])
                ts(norm_adj_T[:], scores[0][:, P:2 * P], degree[:, 0:1], None, ALU.mult).then_inc(setup_done, 1)
                split_weights(BLOCKS_A, len(weight_blocks))
                dve.wait_ge(const_loaded, 16 * len(const_loads))

            split_weights(0, BLOCKS_A)

            def input_lo(s, p):
                dve.wait_ge(xT_hi_ready[s], p + 1)
                tt(xT_lo[s][:].rearrange("p c t -> p (c t)"), bank("xT_" + s)[:],
                   xT_hi[s][:].rearrange("p c t -> p (c t)").bitcast(F32), ALU.subtract).then_inc(emptied["xT_" + s], 1)

            def row_max(s, p, groups):
                for g in groups:
                    dve.wait_ge(scored[s][g], p + 1)
                    nc.vector.tensor_reduce(neg_max[s][:, g, :], scores[g][:].rearrange("p (n k) -> p n k", k=P), AX_X,
                                            ALU.max, negate=True).then_inc(max_ready[s][g], 1)

            def save_q_b(p):
                dve.wait_ge(filled["q_B"], p + 1)
                for c in range(FC):
                    last = ts(qT["B"][:, c].rearrange("p b t -> p (b t)"), bank("q_B")[:, c * NB * P:(c + 1) * NB * P],
                              bq[:, c:c + 1], ATT_SCALE, ALU.add, ALU.mult)
                last.then_inc(emptied["q_B"], 1)

            def invert(s, p, b):
                if b < NB - 1:
                    dve.wait_ge(exp_ready[s][b], p + 1)
                else:
                    dve.wait_ge(scores_read[s][GROUPS - 1], p + 1)
                nc.vector.reciprocal(inv_denom[s][:, b, :], denom[s][:, b, :]).then_inc(inv_ready[s][b], 1)

            def heads_lo(s, p):
                dve.wait_ge(oT_hi_ready[s], p + 1)
                if s == "A":
                    tt(oT_lo[s][:].rearrange("p c b t -> p (c b t)"), bank("o_A")[:],
                       oT_hi[s][:].rearrange("p c b t -> p (c b t)").bitcast(F32), ALU.subtract).then_inc(emptied["o_A"], 1)
                    return
                for c in range(FC):
                    last = stt(out=oT_lo[s][:, c].rearrange("p b t -> p (b t)"),
                               in0=bank("o_B")[:, c * NB * P:(c + 1) * NB * P], scalar=bv[:, c:c + 1],
                               in1=oT_hi[s][:, c].rearrange("p b t -> p (b t)").bitcast(F32),
                               op0=ALU.add, op1=ALU.subtract)
                last.then_inc(emptied["o_B"], 1)

            def statistics(s, p):
                dve.wait_ge(z_of[s], p + 1)
                for b in range(NB):
                    last = nc.vector.bn_stats(stats[s][:, b, :], norm_in[s][:, b, :])
                last.then_inc(stats_ready[s], 1)
                dve.wait_ge(setup_done, 1)
                dve.wait_ge(stats_ready[s], p + 1)
                for b in range(NB):
                    last = nc.vector.bn_aggr(mean_var[s][:, b, :], stats[s][:, b, :])
                last.then_inc(mean_ready[s], 1)
                dve.wait_ge(mean_ready[s], p + 1)
                ts(var_eps[s][:], mean_var[s][:, :, 1], EPS, None, ALU.add).then_inc(var_ready[s], 1)

            def normalise(s, p, taken):
                dve.wait_ge(rstd_ready[s], p + 1)
                for sem_, value in taken:
                    dve.wait_ge(sem_, value)
                for b in range(NB):
                    last = ts(norm_out[s][:, b, :], norm_in[s][:, b, :], mean_var[s][:, b, 0:1], rstd[s][:, b:b + 1],
                              ALU.subtract, ALU.mult)
                last.then_inc(normed[s], 1)

            def add_resid(s, p, name):
                dve.wait_ge(filled[name], p + 1)
                dve.wait_ge(resid_ready[s], p + 1)
                tt(z[s][:].rearrange("p b d -> p (b d)"), bank(name)[:], resid[s][:].rearrange("p b d -> p (b d)"),
                   ALU.add).then_inc(emptied[name], 1)

            def before(sem_, p, one=1):
                return [] if isinstance(p, int) and p == 0 else [(sem_, p * one)]

            def pool_terms(p):
                dve.wait_ge(emptied["pool"], p + 1)
                nc.vector.tensor_reduce(pool_max[:], pooled[:], AX_X, ALU.max)
                stt(out=pool_shift[:].rearrange("p b d -> p (b d)"), in0=pooled[:].rearrange("p b d -> p (b d)"),
                    scalar=b_pool[:, 0:1], in1=pooled[:].rearrange("p b d -> p (b d)"),
                    op0=ALU.add, op1=ALU.subtract).then_inc(pool_shift_ready, 1)

            def pool_layer(p):
                dve.wait_ge(pool_shift_ready, p + 1)
                for b in range(NB):
                    last = ts(pool_relu[:, b, :], pool_shift[:, b, :], pool_max[:, b:b + 1], 0.0, ALU.add, ALU.max)
                last.then_inc(pool_relu_ready, 1)
                dve.wait_ge(pool_relu_ready, p + 1)
                tt(z["D"][:], pool_relu[:], x_in["D"][:], ALU.add).then_inc(z_ready["D"], 1)

            def iteration(i):
                if has(i, 1):
                    dve.wait_ge(filled["proj_A"], i)
                    tt(att_out[:], bank("proj_A")[:].rearrange("p (b d) -> p b d", b=NB), everywhere(b_proj),
                       ALU.add).then_inc(att_out_ready, 1)
                    dve.wait_ge(resid_ready["A"], i)
                    tt(pre_sum[:].rearrange("p b d -> p (b d)"), bank("proj_A")[:],
                       resid["A"][:].rearrange("p b d -> p (b d)"), ALU.add).then_inc(emptied["proj_A"], 1)
                if has(i, 2):
                    invert("B", i - 2, 0)
                if has(i, 1):
                    statistics("I", i - 1)
                if has(i, 4):
                    pool_terms(i - 4)
                if has(i, 2):
                    invert("B", i - 2, 1)
                if has(i, 1):
                    for b in range(NB):
                        last = stt(out=centred[:, b, :], in0=att_out[:, b, :], scalar=mean_var["I"][:, b, 0:1],
                                   in1=gamma[:], op0=ALU.subtract, op1=ALU.mult)
                    last.then_inc(centred_ready, 1)
                if has(i, 1):
                    dve.wait_ge(centred_ready, i)
                    dve.wait_ge(rstd_ready["I"], i)
                    dve.wait_ge(emptied["proj_A"], i)
                    for b in range(NB):
                        last = stt(out=z["A"][:, b, :], in0=centred[:, b, :], scalar=rstd["I"][:, b:b + 1],
                                   in1=pre_sum[:, b, :], op0=ALU.mult, op1=ALU.add)
                    last.then_inc(z_ready["A"], 1)
                    statistics("A", i - 1)
                if has(i, 4):
                    pool_layer(i - 4)
                if has(i, 1):
                    normalise("A", i - 1, before(filled["xT_B"], i - 1) + before(resid_ready["B"], i - 1))
                if has(i, 4):
                    statistics("D", i - 4)
                if has(i, 0):
                    row_max("A", i, range(2))
                if has(i, 2):
                    heads_lo("B", i - 2)
                if has(i, 0):
                    row_max("A", i, range(2, 3))
                if has(i, 1):
                    input_lo("B", i - 1)
                if has(i, 0):
                    row_max("A", i, range(3, GROUPS))
                if has(i, 3):
                    add_resid("C", i - 3, "conv")
                if has(i, 4):
                    normalise("D", i - 4, before(result_stored, i - 4, 16))
                if has(i, 0):
                    invert("A", i, 0)
                if has(i, 1):
                    save_q_b(i - 1)
                if has(i, 2):
                    add_resid("B", i - 2, "proj_B")
                if has(i, 0):
                    invert("A", i, 1)
                if has(i, 2):
                    statistics("B", i - 2)
                if has(i, 3):
                    statistics("C", i - 3)
                if has(i, 2):
                    normalise("B", i - 2, before(filled["mix"], i - 2) + before(resid_ready["C"], i - 2))
                if has(i, 3):
                    normalise("C", i - 3, before(filled["pool"], i - 3) + before(z_ready["D"], i - 3))
                if has(i, 2):
                    dve.wait_ge(mix_hi_ready, i - 1)
                    tt(mixT_lo[:].rearrange("p c b t -> p (c b t)"), bank("mix")[:],
                       mixT_hi[:].rearrange("p c b t -> p (c b t)").bitcast(F32), ALU.subtract).then_inc(emptied["mix"], 1)
                if has(i, 1):
                    row_max("B", i - 1, range(2))
                if has(i, 0):
                    heads_lo("A", i)
                if has(i, 1):
                    row_max("B", i - 1, range(2, 3))
                if has(i, -1):
                    input_lo("A", i + 1)
                if has(i, 1):
                    row_max("B", i - 1, range(3, GROUPS))

            program(iteration, dve, late_setup)

        @block.gpsimd
        def _(pool):
            tt = nc.gpsimd.tensor_tensor
            nc.gpsimd.memset(minus_half[:], -0.5)
            nc.gpsimd.memset(ident[:], 0.0).then_inc(ident_zero, 1)
            pool.wait_ge(ident_zero, 1)
            nc.gpsimd.affine_select(out=ident[:], in_=ident[:], compare_op=ALU.not_equal, fill=1.0, base=0,
                                    pattern=[[-1, P]], channel_multiplier=1).then_inc(ident_ready, 1)
            pool.wait_ge(ident_ready, 1)
            pool.wait_ge(setup_dve, 3)
            tt(degree[:, 3:4], degree[:, 1:2], minus_half[:, 0:1], ALU.pow).then_inc(setup_pow, 1)

            def residual(s, p, ready, value, bias):
                pool.wait_ge(ready, value)
                if not (isinstance(p, int) and p == 0):
                    pool.wait_ge(emptied["conv" if s == "C" else "proj_" + s], p)
                tt(resid[s][:], x_in[s][:], everywhere(bias), ALU.add).then_inc(resid_ready[s], 1)

            def scale_probs(s, p, b):
                pool.wait_ge(inv_ready[s][b], p + 1)
                for c in range(FC):
                    heads = slice(c * GROUPS, (c + 1) * GROUPS)
                    tt(probs[s][:, b, heads], probs[s][:, b, heads],
                       inv_denom[s][:, b, heads].rearrange("p (h o) -> p h o", o=1).to_broadcast([P, GROUPS, P]),
                       ALU.mult).then_inc(probs_ready[s][b * FC + c], 1)

            pool.wait_ge(const_loaded, 16 * len(const_loads))
            tt(b_last[:], beta[:], b_proj[:], ALU.add).then_inc(setup_bias, 1)
            pool.wait_ge(setup_bias, 1)

            def inverse_root(s, p):
                pool.wait_ge(var_ready[s], p + 1)
                tt(rstd[s][:], var_eps[s][:], minus_half[:], ALU.pow).then_inc(rstd_ready[s], 1)

            def iteration(i):
                if has(i, 2):
                    scale_probs("B", i - 2, 0)
                if has(i, 1):
                    inverse_root("I", i - 1)
                if has(i, 2):
                    scale_probs("B", i - 2, 1)
                if has(i, 1):
                    inverse_root("A", i - 1)
                if has(i, 0):
                    residual("A", i, x_loaded, 16 * (i + 1), b_last)
                if has(i, 4):
                    inverse_root("D", i - 4)
                if has(i, 0):
                    scale_probs("A", i, 0)
                if has(i, 0):
                    scale_probs("A", i, 1)
                if has(i, 2):
                    inverse_root("B", i - 2)
                if has(i, 1):
                    residual("B", i - 1, normed["A"], i, b_out)
                if has(i, 3):
                    inverse_root("C", i - 3)
                if has(i, 2):
                    residual("C", i - 2, normed["B"], i - 1, b_conv)

            program(iteration, pool)


_NAMES = ["x", "adj", "L0_gnn_w_qkv", "L0_gnn_w_proj", "L0_gnn_b_proj", "L0_gnn_ln_gamma", "L0_gnn_ln_beta",
          "L1_gnn_Wq", "L1_gnn_bq", "L1_gnn_Wk", "L1_gnn_bk", "L1_gnn_Wv", "L1_gnn_bv", "L1_gnn_Wo", "L1_gnn_bo",
          "L2_gnn_weight", "L2_gnn_bias", "L3_gnn_b"]


def kernel(**inputs):
    import numpy as np
    import concourse.bacc as bacc
    from concourse.bass_utils import run_bass_kernel_spmd

    nc = bacc.Bacc("TRN2", target_bir_lowering=False, num_devices=1)
    arrays, args = {}, {}
    for name in _NAMES:
        arr = np.ascontiguousarray(inputs[name])
        arrays[f"in_{name}"] = arr
        args[name] = nc.dram_tensor(f"in_{name}", arr.shape, mybir.dt.from_np(arr.dtype), kind="ExternalInput").ap()
    shape = arrays["in_x"].shape
    out = nc.dram_tensor("out", shape, F32, kind="ExternalOutput").ap()
    gnn_kernel(nc, args, out, shape[0])
    return run_bass_kernel_spmd(nc, [arrays], core_ids=[0]).results[0]["out"]
```
